# Optimizing a Trainium2 kernel written in Bass

```python
import numpy as np
import jax
import jax.numpy as jnp

def _softmax(x, axis=-1):
    return jax.nn.softmax(x, axis=axis)

def _gelu(x):
    return jax.nn.gelu(x, approximate=True)

def _silu(x):
    return jax.nn.silu(x)

def _sigmoid(x):
    return jax.nn.sigmoid(x)

def _layernorm(x, axis=-1, eps=1e-05):
    m = jnp.mean(x, axis=axis, keepdims=True)
    v = jnp.var(x, axis=axis, keepdims=True)
    return (x - m) / jnp.sqrt(v + eps)

def _scatter_add(tgt, idx, src, axis=0):
    return tgt.at[idx].add(src)

def _segment_sum(src, seg, n):
    return jax.ops.segment_sum(src, seg, n)
kernel_name = 'mk_vit_tower_d1_tok_img1024_r4_acc035'

def setup_inputs(seed: int=0):
    np.random.seed(seed)
    _w = jnp.asarray

    def _rec_inputs():
        import jax
        import jax.numpy as jnp
        _rk = jax.random.key(seed)
        x = -0.000222058 + 0.999998 * jax.random.normal(jax.random.fold_in(_rk, 1), (64, 3, 96, 96), jnp.float32)
        return x
    x = _rec_inputs()

    def _L0_tok_setup():
        import jax, jax.numpy as jnp
        import numpy as np
        P = 16
        C = 3
        D = 256

        def _patchify(x, p):
            B, Cc, H, W = x.shape
            gh, gw = (H // p, W // p)
            x = x.reshape(B, Cc, gh, p, gw, p)
            x = x.transpose(0, 2, 4, 1, 3, 5)
            return x.reshape(B, gh * gw, Cc * p * p)
        key = jax.random.key(seed)
        k1, k2, k3, k4, k5 = jax.random.split(key, 5)
        patch_dim = C * P * P
        s1 = 1.0 / np.sqrt(patch_dim)
        s2 = 1.0 / np.sqrt(D)
        return {'x': jax.random.normal(k1, (32, C, 128, 128), dtype=jnp.float32), 'W1': jax.random.uniform(k2, (patch_dim, D), jnp.float32, -s1, s1), 'b1': jax.random.uniform(k3, (D,), jnp.float32, -s1, s1), 'W2': jax.random.uniform(k4, (D, D), jnp.float32, -s2, s2), 'b2': jax.random.uniform(k5, (D,), jnp.float32, -s2, s2)}
    _L0_tok_all = _L0_tok_setup()
    _L0_tok_in = {k: v for k, v in _L0_tok_all.items() if k in ('W1', 'b1', 'W2', 'b2')}
    del _L0_tok_all

    def _L0_attn_setup():
        import jax, jax.numpy as jnp
        import numpy as np
        D_MODEL = 256
        N_HEADS = 16
        D_HEAD = D_MODEL // N_HEADS
        WINDOW = 64
        key = jax.random.key(seed)
        ks = jax.random.split(key, 9)
        x = jax.random.normal(ks[0], (1, 1024, D_MODEL), dtype=jnp.float32)
        s = 0.02
        params = {'q_w': jax.random.normal(ks[1], (D_MODEL, D_MODEL), jnp.float32) * s, 'q_b': jax.random.normal(ks[2], (D_MODEL,), jnp.float32) * s, 'k_w': jax.random.normal(ks[3], (D_MODEL, D_MODEL), jnp.float32) * s, 'k_b': jax.random.normal(ks[4], (D_MODEL,), jnp.float32) * s, 'v_w': jax.random.normal(ks[5], (D_MODEL, D_MODEL), jnp.float32) * s, 'v_b': jax.random.normal(ks[6], (D_MODEL,), jnp.float32) * s, 'o_w': jax.random.normal(ks[7], (D_MODEL, D_MODEL), jnp.float32) * s, 'o_b': jax.random.normal(ks[8], (D_MODEL,), jnp.float32) * s}
        return {'x': x, **params}
    _L0_attn_all = _L0_attn_setup()
    _L0_attn_in = {k: v for k, v in _L0_attn_all.items() if k in ('q_w', 'q_b', 'k_w', 'k_b', 'v_w', 'v_b', 'o_w', 'o_b')}
    del _L0_attn_all

    def _L0_ffn_setup():
        import jax, jax.numpy as jnp
        import numpy as np
        B, L, D, H, E, K = (4, 512, 256, 512, 8, 2)

        def _mlp(x, w1, b1, w2, b2):
            h = jax.nn.gelu(x @ w1 + b1, approximate=True)
            return h @ w2 + b2
        key = jax.random.key(seed)
        ks = jax.random.split(key, 16)
        s = 0.02
        inp = {'x': jax.random.normal(ks[0], (B, L, D), dtype=jnp.float32), 'task_ids': jax.random.randint(ks[1], (B,), 0, 9), 'gw1': jax.random.normal(ks[2], (D, H), dtype=jnp.float32) * s, 'gb1': jnp.zeros((H,), dtype=jnp.float32), 'gw2': jax.random.normal(ks[3], (H, E), dtype=jnp.float32) * s, 'gb2': jnp.zeros((E,), dtype=jnp.float32), 'We1': jax.random.normal(ks[4], (E, D, H), dtype=jnp.float32) * s, 'be1': jnp.zeros((E, H), dtype=jnp.float32), 'We2': jax.random.normal(ks[5], (E, H, D), dtype=jnp.float32) * s, 'be2': jnp.zeros((E, D), dtype=jnp.float32), 'Ws1': jax.random.normal(ks[6], (D, H), dtype=jnp.float32) * s, 'bs1': jnp.zeros((H,), dtype=jnp.float32), 'Ws2': jax.random.normal(ks[7], (H, D), dtype=jnp.float32) * s, 'bs2': jnp.zeros((D,), dtype=jnp.float32)}
        return inp
    _L0_ffn_all = _L0_ffn_setup()
    _L0_ffn_in = {k: v for k, v in _L0_ffn_all.items() if k in ('task_ids', 'gw1', 'gb1', 'gw2', 'gb2', 'We1', 'be1', 'We2', 'be2', 'Ws1', 'bs1', 'Ws2', 'bs2')}
    del _L0_ffn_all
    return {'x': x, 'L0_tok_W1': _L0_tok_in['W1'], 'L0_tok_b1': _L0_tok_in['b1'], 'L0_tok_W2': _L0_tok_in['W2'], 'L0_tok_b2': _L0_tok_in['b2'], 'L0_attn_q_w': _L0_attn_in['q_w'], 'L0_attn_q_b': _L0_attn_in['q_b'], 'L0_attn_k_w': _L0_attn_in['k_w'], 'L0_attn_k_b': _L0_attn_in['k_b'], 'L0_attn_v_w': _L0_attn_in['v_w'], 'L0_attn_v_b': _L0_attn_in['v_b'], 'L0_attn_o_w': _L0_attn_in['o_w'], 'L0_attn_o_b': _L0_attn_in['o_b'], 'L0_ffn_task_ids': _L0_ffn_in['task_ids'], 'L0_ffn_gw1': _L0_ffn_in['gw1'], 'L0_ffn_gb1': _L0_ffn_in['gb1'], 'L0_ffn_gw2': _L0_ffn_in['gw2'], 'L0_ffn_gb2': _L0_ffn_in['gb2'], 'L0_ffn_We1': _L0_ffn_in['We1'], 'L0_ffn_be1': _L0_ffn_in['be1'], 'L0_ffn_We2': _L0_ffn_in['We2'], 'L0_ffn_be2': _L0_ffn_in['be2'], 'L0_ffn_Ws1': _L0_ffn_in['Ws1'], 'L0_ffn_bs1': _L0_ffn_in['bs1'], 'L0_ffn_Ws2': _L0_ffn_in['Ws2'], 'L0_ffn_bs2': _L0_ffn_in['bs2']}

def reference(x, L0_tok_W1, L0_tok_b1, L0_tok_W2, L0_tok_b2, L0_attn_q_w, L0_attn_q_b, L0_attn_k_w, L0_attn_k_b, L0_attn_v_w, L0_attn_v_b, L0_attn_o_w, L0_attn_o_b, L0_ffn_task_ids, L0_ffn_gw1, L0_ffn_gb1, L0_ffn_gw2, L0_ffn_gb2, L0_ffn_We1, L0_ffn_be1, L0_ffn_We2, L0_ffn_be2, L0_ffn_Ws1, L0_ffn_bs1, L0_ffn_Ws2, L0_ffn_bs2):
    import jax
    import jax.numpy as jnp

    def _L0_tok_ref(x, W1, b1, W2, b2):
        import jax, jax.numpy as jnp
        import numpy as np
        P = 16
        C = 3
        D = 256

        def _patchify(x, p):
            B, Cc, H, W = x.shape
            gh, gw = (H // p, W // p)
            x = x.reshape(B, Cc, gh, p, gw, p)
            x = x.transpose(0, 2, 4, 1, 3, 5)
            return x.reshape(B, gh * gw, Cc * p * p)
        patches = _patchify(x, P)
        h = jax.nn.silu(jnp.einsum('blk,kd->bld', patches, W1) + b1)
        return jnp.einsum('bld,de->ble', h, W2) + b2

    def _L0_attn_ref(x, q_w, q_b, k_w, k_b, v_w, v_b, o_w, o_b):
        import jax, jax.numpy as jnp
        import numpy as np
        D_MODEL = 256
        N_HEADS = 16
        D_HEAD = D_MODEL // N_HEADS
        WINDOW = 64
        B, S, D = x.shape
        scale = jnp.sqrt(jnp.float32(D_HEAD))
        q = (x @ q_w.T + q_b).reshape(B, S, N_HEADS, D_HEAD).transpose(0, 2, 1, 3)
        k = (x @ k_w.T + k_b).reshape(B, S, N_HEADS, D_HEAD).transpose(0, 2, 1, 3)
        v = (x @ v_w.T + v_b).reshape(B, S, N_HEADS, D_HEAD).transpose(0, 2, 1, 3)
        scores = jnp.einsum('bhqd,bhkd->bhqk', q, k) / scale
        idx = jnp.arange(S)
        row = idx[:, None]
        col = idx[None, :]
        masked = (col > row) | (row - col >= min(WINDOW, S))
        scores = jnp.where(masked[None, None], -jnp.inf, scores)
        attn = jax.nn.softmax(scores, axis=-1)
        attn = jnp.nan_to_num(attn, nan=0.0)
        out = jnp.einsum('bhqk,bhkd->bhqd', attn, v)
        out = out.transpose(0, 2, 1, 3).reshape(B, S, D)
        return out @ o_w.T + o_b

    def _L0_ffn_ref(x, task_ids, gw1, gb1, gw2, gb2, We1, be1, We2, be2, Ws1, bs1, Ws2, bs2):
        import jax, jax.numpy as jnp
        import numpy as np
        B, L, D, H, E, K = (4, 512, 256, 512, 8, 2)

        def _mlp(x, w1, b1, w2, b2):
            h = jax.nn.gelu(x @ w1 + b1, approximate=True)
            return h @ w2 + b2
        bsz, length, d = x.shape
        T = bsz * length
        xf = x.reshape(T, d)
        logits = jax.nn.gelu(xf @ gw1 + gb1, approximate=False) @ gw2 + gb2
        scores = jax.nn.softmax(logits, axis=-1)
        topk_w, topk_idx = jax.lax.top_k(scores, K)
        rows = jnp.arange(T)[:, None]
        gates = jnp.zeros_like(scores).at[rows, topk_idx].set(topk_w)
        out = _mlp(xf, Ws1, bs1, Ws2, bs2)
        for e in range(E):
            out = out + gates[:, e:e + 1] * _mlp(xf, We1[e], be1[e], We2[e], be2[e])
        return out.reshape(bsz, length, d)
    h = _L0_tok_ref(x, L0_tok_W1, L0_tok_b1, L0_tok_W2, L0_tok_b2)
    h = h + _L0_attn_ref(_layernorm(h, axis=-1), L0_attn_q_w, L0_attn_q_b, L0_attn_k_w, L0_attn_k_b, L0_attn_v_w, L0_attn_v_b, L0_attn_o_w, L0_attn_o_b)
    h = h + _L0_ffn_ref(_layernorm(h, axis=-1), L0_ffn_task_ids, L0_ffn_gw1, L0_ffn_gb1, L0_ffn_gw2, L0_ffn_gb2, L0_ffn_We1, L0_ffn_be1, L0_ffn_We2, L0_ffn_be2, L0_ffn_Ws1, L0_ffn_bs1, L0_ffn_Ws2, L0_ffn_bs2)
    return h

_drawn_inputs = setup_inputs


def setup_inputs(seed=0):
    import zlib

    import numpy as np

    out = dict(_drawn_inputs(seed))
    spreads = {'L0_ffn_gb1': (0.0, 0.1),
     'L0_ffn_gb2': (0.0, 0.1),
     'L0_ffn_be1': (0.0, 0.366),
     'L0_ffn_be2': (0.0, 0.1),
     'L0_ffn_bs1': (0.0, 0.1),
     'L0_ffn_bs2': (0.0, 0.1)}
    factors = {'L0_attn_q_w': 3.002, 'L0_attn_q_b': 8.0, 'L0_attn_k_w': 3.361, 'L0_attn_k_b': 8.0}
    for name, (base, spread) in spreads.items():
        noise = np.random.default_rng([zlib.crc32(name.encode()), seed]).standard_normal(out[name].shape)
        drawn = base * np.exp(spread * noise) if base else spread * noise
        out[name] = jnp.asarray(drawn.astype(out[name].dtype))
    for name, factor in factors.items():
        out[name] = (out[name] * factor).astype(out[name].dtype)
    return out
```

```python
import concourse.bass as bass
from concourse import mybir
from contextlib import ExitStack

F32 = mybir.dt.float32
BF16 = mybir.dt.bfloat16
I32 = mybir.dt.int32
U32 = mybir.dt.uint32
ALU = mybir.AluOpType
ACT = mybir.ActivationFunctionType
AX = mybir.AxisListType
ds = bass.ds

P = 128
IMAGES, SEQ = 64, 36
D = 256
CD = D // P
KP = 768 // P
H, DH = 16, 16
HC = H // CD
HID = 512
CH = HID // P
E = 8
T = IMAGES * SEQ
NG = 3 * SEQ
GROUPS = -(-IMAGES // 3)
NL = T - (GROUPS - 1) * NG
ROW = D + 2
REGION = T + P
DUMMY = E * REGION
TILES = 2 * T // P + E - 1
EPS = 1e-5
QUART = 4

C_ID = 0
C_MASK = C_ID + P
C_HEAD = C_MASK + NG
C_TRI = C_HEAD + HC
C_IOTA = C_TRI + P
C_BASE = C_IOTA + E
C_LT = C_BASE + E
C_J = C_LT + E * E
C_TOK = C_J + TILES * E
C_PADT = C_TOK + GROUPS
C_N = C_PADT + 1


class Group:

    def __init__(self, turns, turn, r, count):
        self.turns, self.turn, self.r = turns, turn, r
        self.g = turn * turns + r
        self.par = r % 2
        known = isinstance(self.g, int)
        self.exists = not known or 0 <= self.g < count
        self.n = NL if known and self.g == GROUPS - 1 else NG

    def use(self, slots):
        return self.turn * (self.turns // slots) + self.r // slots + 1


def wait(engine, semaphore, value):
    if isinstance(value, int) and value <= 0:
        return
    engine.wait_ge(semaphore, value)


def wait_alone(engine, semaphore, value):
    if isinstance(value, int) and value <= 0:
        return
    engine.wait_ge(semaphore, value)
    if not isinstance(value, int):
        engine.nop(nofuse=True)


def pipeline(engine, step, depth, count=GROUPS, turns=2):
    start = -(-(depth + 2) // turns) * turns
    stop = (count - 1) // turns * turns

    def run(turn, u):
        step(lambda s: Group(turns, turn + (u - s) // turns, (u - s) % turns, count))

    for t in range(start):
        run(t // turns, t % turns)
    with engine.Fori(start // turns, stop // turns) as turn:
        for u in range(turns):
            run(turn, u)
    for t in range(stop, count + depth):
        run(t // turns, t % turns)


def spread(ap, shape):
    return ap.unsqueeze(1).broadcast_to(shape)


def spread_in(ap, shape):
    return ap.unsqueeze(2).broadcast_to(shape)


ROUTE, SLOT = 15, 4


def vit_kernel(nc, a):
    ctx = ExitStack()
    with ctx:
        def sb(name, shape, dt=F32):
            return ctx.enter_context(nc.sbuf_tensor(name, shape, dt))

        def sem(name):
            return ctx.enter_context(nc.semaphore(name))

        const = sb("const", [P, C_N])
        ident = const[:, C_ID:C_ID + P]
        tri = const[:, C_TRI:C_TRI + P]
        ident_bf = sb("ident_bf", [P, NG], BF16)
        mask_bf = sb("mask_bf", [P, NG], BF16)
        ones = sb("ones", [P, P])
        tokw = sb("tokw", [P, (KP + CD) * D])
        w1 = tokw[:, 0:KP * D].rearrange("p (k n) -> p k n", k=KP)
        w2 = tokw[:, KP * D:].rearrange("p (k n) -> p k n", k=CD)
        wqk = sb("wqk", [P, CD, 2 * D])
        wv = sb("wv", [P, CD, D])
        wo = sb("wo", [P, CD, D])
        gw1 = sb("gw1", [P, CD, HID])
        gw2 = sb("gw2", [P, CH, E])
        ws1 = sb("ws1", [P, CD, HID])
        ws2 = sb("ws2", [P, CH, D])
        cols = sb("cols", [P, CD + 2 * CD + 2 * CH])
        b1c, qkbc = cols[:, 0:CD], cols[:, CD:3 * CD]
        gb1c, bs1c = cols[:, 3 * CD:3 * CD + CH], cols[:, 3 * CD + CH:]
        rows = sb("rows", [P, 4 * D + E])
        b2r, vbr, obr, bs2r = (rows[:, i * D:(i + 1) * D] for i in range(4))
        gb2r = rows[:, 4 * D:]
        we1 = sb("we1", [P, E * CD * HID])
        resid = sb("resid", [P, GROUPS * D])
        routed = sb("routed", [P, GROUPS * D])
        xn2t_all = sb("xn2t_all", [P, CD, T])
        expo = sb("expo", [P, 1])

        arena = sb("arena", [P, E * CH * D + E * HID + E * D])
        we2 = arena[:, 0:E * CH * D]
        be1r = arena[:, E * CH * D:E * CH * D + E * HID]
        be2r = arena[:, E * CH * D + E * HID:]
        used = [0]

        def piece(*shape):
            n = 1
            for s in shape:
                n *= s
            v = arena[:, used[0]:used[0] + n]
            used[0] += n
            assert used[0] <= E * CH * D + E * HID + E * D
            names = "abc"[:len(shape)]
            if len(shape) == 1:
                return v
            return v.rearrange(f"p ({' '.join(names)}) -> p {' '.join(names)}",
                               **{names[i]: shape[i] for i in range(len(shape) - 1)})

        def pair(*shape):
            return [piece(*shape), piece(*shape)]

        km = pair(CD * HC, NG)
        prob = piece(H, NG)
        prob_t = piece(H, NG)
        diff = pair(QUART, NG)
        patch = pair(KP, NG)
        q_t = pair(CD, NG)

        pre = sb("pre", [P, CD, NG])
        tanh_h = sb("tanh_h", [P, CD, NG])
        silu = sb("silu", [P, CD, NG])
        tok = sb("tok", [P, D])
        stat = sb("stat", [P, 2, 6])
        mv = sb("mv", [P, 2, 2])
        rstd = sb("rstd", [P, 2, 1])
        xn = sb("xn", [P, D])
        xn_t = sb("xn_t", [P, CD, NG])
        k_t = sb("k_t", [P, CD, NG])
        v_ext = [sb(f"v_ext{i}", [P, H, DH + 1]) for i in range(2)]
        smax = sb("smax", [P, QUART])
        rsum = sb("rsum", [P, H, 1])
        att = sb("att", [P, D])
        att_t = sb("att_t", [P, CD, NG])
        xn2 = sb("xn2", [P, D])

        gh = [wqk[:, i, 0:CH * NG].rearrange("p (c n) -> p c n", c=CH) for i in range(2)]
        logit = sb("logit", [P, E])
        top = sb("top", [P, E])
        topi = sb("topi", [P, E], U32)
        topf = sb("topf", [P, 2])
        hot = [sb(f"hot{i}", [P, 2, E]) for i in range(2)]
        chosen = [sb(f"chosen{i}", [P, E]) for i in range(2)]
        before = [sb(f"before{i}", [P, E]) for i in range(2)]
        slot_of = sb("slot_of", [P, E])
        slot_tmp = sb("slot_tmp", [P, 2, E])
        slot_f = sb("slot_f", [P, 2])
        slot_i = [sb(f"slot_i{i}", [P, 2], U32) for i in range(2)]
        gap = sb("gap", [P, E])
        half_tanh = sb("half_tanh", [P, E])
        num = sb("num", [P, E])
        den = sb("den", [P, E])
        gsum = sb("gsum", [P, 1])
        gates = [sb(f"gates{i}", [P, 2]) for i in range(2)]
        sent = [[sb(f"sent{k}{i}", [P, ROW]) for i in range(2)] for k in range(2)]
        pad = sb("pad", [P, ROW])

        tf = tokw[0:1, 0:8 * E + 5 * TILES * E]
        counts, ntile, start_t, end_t = (tf[:, i * E:(i + 1) * E] for i in range(4))
        wt = tf[:, 4 * E:5 * E]
        tb = [tf[:, 8 * E + i * TILES * E:8 * E + (i + 1) * TILES * E].rearrange("p (j e) -> p j e", e=E)
              for i in range(5)]
        table_f = sb("table_f", [1, 3 * TILES])
        table = sb("table", [1, 2 * TILES], I32)
        count_i = sb("count_i", [1, 2 * E], I32)
        lt_tmp = sb("lt_tmp", [1, E * E])

        left = [0]

        def late(*shape):
            n = shape[0] * (shape[1] if len(shape) > 1 else 1)
            v = routed[:, left[0]:left[0] + n]
            left[0] += n
            assert left[0] <= GROUPS * D
            return v if len(shape) == 1 else v.rearrange("p (c n) -> p c n", c=shape[0])

        xe = [late(ROW) for i in range(4)]
        xe_t = [late(CD, P) for i in range(2)]
        epre = late(HID)
        ehid = [late(HID) for i in range(2)]
        ehid_t = [late(CH, P) for i in range(2)]
        ey = late(D)
        eout = [late(D) for i in range(2)]
        etok = [sb(f"etok{i}", [P, 1], U32) for i in range(2)]

        bank = [ctx.enter_context(nc.psum_tensor(f"bank{i}", [P, 512], F32)) for i in range(8)]

        def view(b, c, n):
            return bank[b][:, 0:c * NG].rearrange("p (c n) -> p c n", n=NG)[:, :, 0:n]

        S = {name: sem(name) for name in """
            const_in w1_in w2_in wqk_in wv_in wo_in cols_in rows_in gw1_in gw2_in ws1_in ws2_in we1_in late_in
            patch0_in patch1_in prep_dve prep_steps before_set pool_steps
            emb_done pre_done tanh_done silu_done tok_done ln1_stat ln1_rstd ln1_done base_done t1_done xnt_ready
            qk_done v_done q_ready k_ready km_ready v_ready score_done smax_done diff_done exp_done pt_done
            probt_ready pv_done rsum_done att_done t2_done attt_ready o_done x1_done ln2_stat ln2_rstd ln2_done
            t3_done xn2t_ready routed_ready
            gh_done gelu_done logit_done route htanh_done rank_done scatter0 scatter1 slot_steps sent_ready totals_done table_steps tabled pad_set pads_in padacc_in
            sh_done shgelu_done so_done acc_ready acc_in
            xe0_in xe1_in xe2_in xe3_in xet_done xet_ready eh_done epre_done egelu_done eht_done eht_ready
            ey_done eyb_done eout_ready ey_steps added out_done
        """.split()}

        block = ctx.enter_context(nc.Block())

        @block.sync
        def _(sp):
            def load(dst, src, s, n=16):
                sp.dma_start(dst, src).then_inc(S[s], 16)

            load(w1, a["w1"], "w1_in")

            def load_patch(G):
                if not G.exists:
                    return
                wait(sp, S["emb_done"], G.g - 1)
                if G.n == NG:
                    src = a["patch"][ds(G.g * P, P), :]
                else:
                    src = a["patch_last"]
                dst = patch[G.par][:, :, 0:G.n]
                sp.dma_start(dst, src.rearrange("p (k n) -> p k n", k=KP)).then_inc(S[f"patch{G.par}_in"], 16)

            load_patch(Group(2, 0, 0, GROUPS))
            load(cols[:], a["cols"], "cols_in")
            load(const[:], a["const"], "const_in")
            load(w2, a["w2"], "w2_in")
            load(rows[:], a["rows"].broadcast_to([P, 4 * D + E]), "rows_in")
            load_patch(Group(2, 0, 1, GROUPS))
            load(wqk[:], a["wqk"], "wqk_in")
            load(wv[:], a["wv"], "wv_in")
            load(wo[:], a["wo"], "wo_in")

            def step(at):
                G = at(0)
                if isinstance(G.g, int) and G.g < 2:
                    return
                load_patch(G)

            pipeline(sp, step, 0)
            load(gw1[:], a["gw1"], "gw1_in")
            load(gw2[:], a["gw2"], "gw2_in")
            load(ws1[:], a["ws1"], "ws1_in")
            load(ws2[:], a["ws2"], "ws2_in")
            load(we1[:], a["we1"], "we1_in")
            sp.wait_ge(S["pv_done"], GROUPS)
            load(we2, a["we2"], "late_in")
            load(be1r, a["be1"].broadcast_to([P, E * HID]), "late_in")
            load(be2r, a["be2"].broadcast_to([P, E * D]), "late_in")
            sp.wait_ge(S["pad_set"], 1)
            sp.dma_start(a["slots"][DUMMY:DUMMY + P, :], pad[:]).then_inc(S["pads_in"], 16)
            sp.dma_start(a["acc"][T:T + P, :], pad[:, 0:D]).then_inc(S["acc_in"], 16)
            sp.wait_ge(S["tabled"], 1)
            for e in range(E):
                c = sp.value_load(count_i[0:1, e:e + 1], min_val=0, max_val=T)
                sp.dma_start(a["slots"][ds(c + e * REGION, P), :], pad[:]).then_inc(S["pads_in"], 16)
            sp.wait_ge(S["pads_in"], 16 * (E + 1))
            sp.wait_ge(S["scatter0"], 16 * 2 * (GROUPS // 2))
            sp.wait_ge(S["scatter1"], 16 * 2 * (GROUPS // 2))

            def tile_load(j, u):
                r = sp.value_load(table[0:1, ds(j, 1)], min_val=0, max_val=DUMMY)
                wait(sp, S["added"], (j - 3) * 16)
                sp.dma_start(xe[u], a["slots"][ds(r, P), :]).then_inc(S[f"xe{u}_in"], 16)

            for j in range(4):
                tile_load(j, j)
            with sp.Fori(1, TILES // 4) as q:
                for u in range(4):
                    tile_load(q * 4 + u, u)
            for j in range(TILES // 4 * 4, TILES):
                tile_load(j, j % 4)
            sp.wait_ge(S["added"], 16 * TILES)

        @block.tensor
        def _(pe):
            mm = nc.tensor.matmul

            def embed(G):
                n = G.n
                pe.wait_ge(S[f"patch{G.par}_in"], 16 * G.use(2))
                wait(pe, S["xnt_ready"], G.g)
                for m in range(CD):
                    for k in range(KP):
                        last = mm(bank[4][:, m * NG:m * NG + n], w1[:, k, m * P:(m + 1) * P],
                                  patch[G.par][:, k, 0:n], start=k == 0, stop=k == KP - 1)
                last.then_inc(S["emb_done"], 1)

            def token(G):
                n = G.n
                pe.wait_ge(S["silu_done"], G.g + 1)
                wait(pe, S["v_ready"], G.g)
                for c in range(CD):
                    last = mm(bank[5][0:n, 0:D], silu[:, c, 0:n], w2[:, c, :], start=c == 0, stop=c == CD - 1)
                last.then_inc(S["tok_done"], 1)

            def norm1_t(G):
                n = G.n
                pe.wait_ge(S["ln1_done"], G.g + 1)
                for c in range(CD):
                    last = nc.tensor.transpose(bank[4][:, c * NG:c * NG + n], xn[0:n, c * P:(c + 1) * P],
                                               ident[0:n, 0:n])
                last.then_inc(S["t1_done"], 1)

            def qkv(G):
                n = G.n
                pe.wait_ge(S["xnt_ready"], G.g + 1)
                wait(pe, S["k_ready"], G.g)
                wait(pe, S["xn2t_ready"], G.g - 1)
                for m in range(2 * CD):
                    for k in range(CD):
                        last = mm(bank[6][:, m * NG:m * NG + n], wqk[:, k, m * P:(m + 1) * P], xn_t[:, k, 0:n],
                                  start=k == 0, stop=k == CD - 1)
                last.then_inc(S["qk_done"], 1)
                for k in range(CD):
                    last = mm(bank[5][0:n, 0:D], xn_t[:, k, 0:n], wv[:, k, :], start=k == 0, stop=k == CD - 1)
                last.then_inc(S["v_done"], 1)

            def scores(G):
                n = G.n
                pe.wait_ge(S["q_ready"], G.g + 1)
                pe.wait_ge(S["km_ready"], G.g + 1)
                for j in range(H // QUART):
                    wait(pe, S["probt_ready"], (G.g - 1) * 4 + j + 1)
                    o = view(j, QUART, n)[0:n]
                    c = j * QUART // HC
                    mm(o, q_t[G.par][:, c, 0:n], km[G.par][:, j * QUART:(j + 1) * QUART, 0:n], start=True, stop=False)
                    m = spread(mask_bf[0:n, 0:n], [n, QUART, n])
                    mm(o, ident_bf[0:n, 0:n], m, start=False, stop=True).then_inc(S["score_done"], 1)

            def probs_t(G):
                n = G.n
                for j in range(H // QUART):
                    pe.wait_ge(S["exp_done"], G.g * 4 + j + 1)
                    for i in range(QUART):
                        last = nc.tensor.transpose(bank[j][0:n, i * NG:i * NG + n], prob[0:n, j * QUART + i, 0:n],
                                                   ident[0:n, 0:n])
                    last.then_inc(S["pt_done"], 1)

            def values(G):
                n = G.n
                pe.wait_ge(S["probt_ready"], G.g * 4 + 4)
                pe.wait_ge(S["v_ready"], G.g + 1)
                wait(pe, S["x1_done"], G.g)
                for h in range(H):
                    last = mm(bank[7][0:n, h * (DH + 1):(h + 1) * (DH + 1)], prob_t[0:n, h, 0:n],
                              v_ext[G.par][0:n, h, :], start=True, stop=True)
                last.then_inc(S["pv_done"], 1)

            def att_trans(G):
                n = G.n
                pe.wait_ge(S["att_done"], G.g + 1)
                wait(pe, S["xn2t_ready"], G.g)
                nxt = min(G.g + 2, GROUPS) if isinstance(G.g, int) else G.g + 2
                pe.wait_ge(S["k_ready"], nxt)
                for c in range(CD):
                    last = nc.tensor.transpose(bank[6][:, c * NG:c * NG + n], att[0:n, c * P:(c + 1) * P],
                                               ident[0:n, 0:n])
                last.then_inc(S["t2_done"], 1)

            def project(G):
                n = G.n
                pe.wait_ge(S["attt_ready"], G.g + 1)
                for c in range(CD):
                    last = mm(bank[7][0:n, 0:D], att_t[:, c, 0:n], wo[:, c, :], start=c == 0, stop=c == CD - 1)
                last.then_inc(S["o_done"], 1)

            def norm2_t(G):
                n = G.n
                pe.wait_ge(S["ln2_done"], G.g + 1)
                for c in range(CD):
                    last = nc.tensor.transpose(bank[6][:, c * NG:c * NG + n], xn2[0:n, c * P:(c + 1) * P],
                                               ident[0:n, 0:n])
                last.then_inc(S["t3_done"], 1)

            def step_a(at):
                new, mid, old = at(0), at(1), at(2)
                if new.exists:
                    embed(new)
                if old.exists:
                    att_trans(old)
                if mid.exists:
                    scores(mid)
                if new.exists:
                    token(new)
                if old.exists:
                    project(old)
                if mid.exists:
                    probs_t(mid)
                if new.exists:
                    norm1_t(new)
                if mid.exists:
                    values(mid)
                if old.exists:
                    norm2_t(old)
                if new.exists:
                    qkv(new)

            for s in "w1_in const_in w2_in wqk_in wv_in wo_in".split():
                pe.wait_ge(S[s], 16)
            pe.wait_ge(S["prep_dve"], 1)
            pipeline(pe, step_a, 2)

            def route_hidden(G):
                n = G.n
                wait(pe, S["gelu_done"], G.g - 1)
                for m in range(CH):
                    for k in range(CD):
                        last = mm(bank[G.par][:, m * NG:m * NG + n], gw1[:, k, m * P:(m + 1) * P],
                                  xn2t_all[:, k, ds(G.g * NG, n)], start=k == 0, stop=k == CD - 1)
                last.then_inc(S["gh_done"], 1)

            def route_logits(G):
                n = G.n
                pe.wait_ge(S["gelu_done"], G.g + 1)
                wait(pe, S["route"], (G.g - 1) * ROUTE + 1)
                for c in range(CH):
                    last = mm(bank[2][0:n, 0:E], gh[G.par][:, c, 0:n], gw2[:, c, :], start=c == 0, stop=c == CH - 1)
                last.then_inc(S["logit_done"], 1)

            def route_rank(G):
                n = G.n
                pe.wait_ge(S["route"], G.g * ROUTE + 7)
                wait(pe, S["slot_steps"], (G.g - 1) * SLOT + 1)
                mm(bank[3][0:n, 0:E], tri[0:n, 0:n], chosen[G.par][0:n, :], start=True, stop=False)
                mm(bank[3][0:n, 0:E], ones[:, 0:n], before[G.par][:, :], start=False, stop=True).then_inc(
                    S["rank_done"], 1)

            def step_b(at):
                new, mid, old = at(0), at(1), at(2)
                if new.exists:
                    route_hidden(new)
                if mid.exists:
                    route_logits(mid)
                if old.exists:
                    route_rank(old)

            pe.wait_ge(S["gw1_in"], 16)
            pe.wait_ge(S["gw2_in"], 16)
            pe.wait_ge(S["before_set"], 1)
            pe.wait_ge(S["xn2t_ready"], GROUPS)
            pe.wait_ge(S["probt_ready"], 4 * GROUPS)
            pipeline(pe, step_b, 2)
            pe.wait_ge(S["slot_steps"], (GROUPS - 1) * SLOT + 1)
            pe.wait_ge(S["route"], GROUPS * ROUTE)
            mm(bank[3][0:1, 0:E], ones[:, 0:1], before[GROUPS % 2][:, :], start=True, stop=True).then_inc(
                S["totals_done"], 1)

            def shared_hidden(G):
                n = G.n
                wait(pe, S["shgelu_done"], G.g - 1)
                for m in range(CH):
                    for k in range(CD):
                        last = mm(bank[G.par][:, m * NG:m * NG + n], ws1[:, k, m * P:(m + 1) * P],
                                  xn2t_all[:, k, ds(G.g * NG, n)], start=k == 0, stop=k == CD - 1)
                last.then_inc(S["sh_done"], 1)

            def shared_out(G):
                n = G.n
                pe.wait_ge(S["shgelu_done"], G.g + 1)
                wait(pe, S["acc_ready"], G.g - 1)
                for c in range(CH):
                    last = mm(bank[4 + G.par][0:n, 0:D], gh[G.par][:, c, 0:n], ws2[:, c, :],
                              start=c == 0, stop=c == CH - 1)
                last.then_inc(S["so_done"], 1)

            def step_c(at):
                if at(0).exists:
                    shared_hidden(at(0))
                if at(1).exists:
                    shared_out(at(1))

            pe.wait_ge(S["ws1_in"], 16)
            pe.wait_ge(S["ws2_in"], 16)
            pe.wait_ge(S["gelu_done"], GROUPS)
            pipeline(pe, step_c, 1)

            pe.wait_ge(S["tabled"], 1)
            pe.wait_ge(S["we1_in"], 16)
            pe.wait_ge(S["late_in"], 48)
            pe.wait_ge(S["shgelu_done"], GROUPS)
            pe.wait_ge(S["acc_ready"], GROUPS)

            def expert_of(G):
                return pe.value_load(table[0:1, ds(G.g + TILES, 1)], min_val=0, max_val=E - 1)

            def rows_t(G):
                u4 = G.r
                wait(pe, S["xet_ready"], G.g - 1)
                pe.wait_ge(S[f"xe{u4}_in"], 16 * G.use(4))
                for c in range(CD):
                    last = nc.tensor.transpose(bank[G.par][:, c * P:(c + 1) * P], xe[u4][:, c * P:(c + 1) * P],
                                               ident[:, :])
                last.then_inc(S["xet_done"], 1)

            def up(G):
                e = expert_of(G)
                pe.wait_ge(S["xet_ready"], G.g + 1)
                wait(pe, S["epre_done"], G.g - 1)
                for k in range(CD):
                    last = mm(bank[2 + G.par][:, :], xe_t[G.par][:, k, :], we1[:, ds(e * (CD * HID) + k * HID, HID)],
                              start=k == 0, stop=k == CD - 1)
                last.then_inc(S["eh_done"], 1)

            def hidden_t(G):
                pe.wait_ge(S["egelu_done"], G.g + 1)
                wait(pe, S["eht_ready"], G.g - 1)
                for c in range(CH):
                    last = nc.tensor.transpose(bank[4 + G.par][:, c * P:(c + 1) * P], ehid[G.par][:, c * P:(c + 1) * P],
                                               ident[:, :])
                last.then_inc(S["eht_done"], 1)

            def down(G):
                e = expert_of(G)
                pe.wait_ge(S["eht_ready"], G.g + 1)
                wait(pe, S["ey_steps"], (G.g - 2) * 3 + 1)
                for c in range(CH):
                    last = mm(bank[6 + G.par][:, 0:D], ehid_t[G.par][:, c, :], we2[:, ds(e * (CH * D) + c * D, D)],
                              start=c == 0, stop=c == CH - 1)
                last.then_inc(S["ey_done"], 1)

            def step_d(at):
                if at(1).exists:
                    up(at(1))
                if at(0).exists:
                    rows_t(at(0))
                if at(3).exists:
                    down(at(3))
                if at(2).exists:
                    hidden_t(at(2))

            pipeline(pe, step_d, 3, TILES, 4)

        @block.scalar
        def _(act):
            def act_tanh(G):
                wait(act, S["silu_done"], G.g)
                act.wait_ge(S["pre_done"], G.g + 1)
                nc.scalar.activation(tanh_h[:, :, 0:G.n], pre[:, :, 0:G.n], ACT.Tanh, scale=0.5).then_inc(
                    S["tanh_done"], 1)

            def act_attt(G):
                act.wait_ge(S["t2_done"], G.g + 1)
                nc.scalar.copy(att_t[:, :, 0:G.n], view(6, CD, G.n)).then_inc(S["attt_ready"], 1)

            def act_exp(G, j):
                n = G.n
                act.wait_ge(S["diff_done"], G.g * 4 + j + 1)
                wait(act, S["pt_done"], (G.g - 1) * 4 + j + 1)
                nc.scalar.activation(prob[0:n, j * QUART:(j + 1) * QUART, 0:n], diff[j % 2][0:n, :, 0:n], ACT.Exp,
                                     scale=DH ** -0.5).then_inc(S["exp_done"], 1)

            def act_probt(G, j):
                n = G.n
                act.wait_ge(S["pt_done"], G.g * 4 + j + 1)
                wait(act, S["pv_done"], G.g)
                nc.scalar.copy(prob_t[0:n, j * QUART:(j + 1) * QUART, 0:n], view(j, QUART, n)[0:n]).then_inc(
                    S["probt_ready"], 1)

            def act_xnt(G):
                act.wait_ge(S["t1_done"], G.g + 1)
                nc.scalar.copy(xn_t[:, :, 0:G.n], view(4, CD, G.n)).then_inc(S["xnt_ready"], 1)

            def act_xn2t(G):
                act.wait_ge(S["t3_done"], G.g + 1)
                nc.scalar.copy(xn2t_all[:, :, ds(G.g * NG, G.n)], view(6, CD, G.n)).then_inc(S["xn2t_ready"], 1)

            def act_qk(G):
                n = G.n
                act.wait_ge(S["qk_done"], G.g + 1)
                for c in range(CD):
                    last = nc.scalar.activation(q_t[G.par][:, c, 0:n], bank[6][:, c * NG:c * NG + n], ACT.Identity,
                                                bias=qkbc[:, c:c + 1])
                last.then_inc(S["q_ready"], 1)
                wait(act, S["km_ready"], G.g)
                for c in range(CD):
                    m = CD + c
                    last = nc.scalar.activation(k_t[:, c, 0:n], bank[6][:, m * NG:m * NG + n], ACT.Identity,
                                                bias=qkbc[:, m:m + 1])
                last.then_inc(S["k_ready"], 1)

            def step_a(at):
                new, mid, old = at(0), at(1), at(2)
                if new.exists:
                    act_tanh(new)
                if old.exists:
                    act_attt(old)
                if mid.exists:
                    act_exp(mid, 0)
                    act_exp(mid, 1)
                    act_exp(mid, 2)
                    act_probt(mid, 0)
                    act_exp(mid, 3)
                    act_probt(mid, 1)
                    act_probt(mid, 2)
                    act_probt(mid, 3)
                if new.exists:
                    act_xnt(new)
                if old.exists:
                    act_xn2t(old)
                if new.exists:
                    act_qk(new)

            act.wait_ge(S["cols_in"], 16)
            pipeline(act, step_a, 2)

            def act_gelu(G):
                n = G.n
                act.wait_ge(S["gh_done"], G.g + 1)
                wait(act, S["logit_done"], G.g - 1)
                for m in range(CH):
                    last = nc.scalar.activation(gh[G.par][:, m, 0:n], bank[G.par][:, m * NG:m * NG + n], ACT.Gelu,
                                                bias=gb1c[:, m:m + 1])
                last.then_inc(S["gelu_done"], 1)

            def act_half_tanh(G):
                n = G.n
                act.wait_ge(S["route"], G.g * ROUTE + 9)
                nc.scalar.activation(half_tanh[0:n, :], gap[0:n, :], ACT.Tanh, scale=0.5).then_inc(
                    S["htanh_done"], 1)

            def step_b(at):
                if at(0).exists:
                    act_gelu(at(0))
                if at(1).exists:
                    act_half_tanh(at(1))

            pipeline(act, step_b, 2)

            def act_shared(G):
                n = G.n
                act.wait_ge(S["sh_done"], G.g + 1)
                act.wait_ge(S["logit_done"], GROUPS)
                wait(act, S["so_done"], G.g - 1)
                for m in range(CH):
                    last = nc.scalar.activation(gh[G.par][:, m, 0:n], bank[G.par][:, m * NG:m * NG + n],
                                                ACT.Gelu_apprx_tanh, bias=bs1c[:, m:m + 1])
                last.then_inc(S["shgelu_done"], 1)

            def acc_store(G):
                act.wait_ge(S["acc_ready"], G.g + 1)
                act.dma_start(a["acc"][ds(G.g * NG, G.n), :], resid[0:G.n, ds(G.g * D, D)]).then_inc(S["acc_in"], 16)

            def step_c(at):
                if at(0).exists:
                    act_shared(at(0))
                if at(2).exists:
                    acc_store(at(2))

            pipeline(act, step_c, 2)

            def act_rows(G):
                act.wait_ge(S["xet_done"], G.g + 1)
                nc.scalar.copy(xe_t[G.par][:, :, :], bank[G.par][:, 0:D].rearrange("p (c n) -> p c n", c=CD)).then_inc(
                    S["xet_ready"], 1)

            def act_egelu(G):
                act.wait_ge(S["epre_done"], G.g + 1)
                wait(act, S["eht_done"], G.g - 1)
                nc.scalar.activation(ehid[G.par][:, :], epre[:, :], ACT.Gelu_apprx_tanh).then_inc(S["egelu_done"], 1)

            def step_d(at):
                if at(0).exists:
                    act_rows(at(0))
                if at(1).exists:
                    act_egelu(at(1))

            pipeline(act, step_d, 3, TILES, 4)

        @block.vector
        def _(dve):
            V = nc.vector

            dve.wait_ge(S["const_in"], 16)
            V.tensor_copy(ident_bf[:], const[:, C_ID:C_ID + NG])
            V.tensor_copy(mask_bf[:], const[:, C_MASK:C_MASK + NG])
            dve.wait_ge(S["w2_in"], 16)
            V.tensor_scalar(w2, w2, 0.5, None, ALU.mult)
            V.memset(v_ext[0][:, :, DH:DH + 1], 1.0)
            V.memset(v_ext[1][:, :, DH:DH + 1], 1.0)
            V.memset(ones[:], 1.0).then_inc(S["prep_dve"], 1)

            def dve_silu(G):
                n = G.n
                dve.wait_ge(S["emb_done"], G.g + 1)
                wait(dve, S["tanh_done"], G.g)
                for m in range(CD):
                    last = V.tensor_scalar(pre[:, m, 0:n], bank[4][:, m * NG:m * NG + n], b1c[:, m:m + 1], None,
                                           ALU.add)
                last.then_inc(S["pre_done"], 1)
                dve.wait_ge(S["tanh_done"], G.g + 1)
                wait(dve, S["tok_done"], G.g)
                V.scalar_tensor_tensor(out=silu[:, :, 0:n], in0=tanh_h[:, :, 0:n], scalar=1.0, in1=pre[:, :, 0:n],
                                       op0=ALU.add, op1=ALU.mult).then_inc(S["silu_done"], 1)

            def softmax(G, j):
                n = G.n
                dve.wait_ge(S["score_done"], G.g * 4 + j + 1)
                s = view(j, QUART, n)[0:n]
                wait(dve, S["diff_done"], G.g * 4 + j)
                V.reduce_max(smax[0:n, :], s, AX.X).then_inc(S["smax_done"], 1)
                dve.wait_ge(S["smax_done"], G.g * 4 + j + 1)
                wait(dve, S["exp_done"], G.g * 4 + j - 1)
                V.tensor_tensor(diff[j % 2][0:n, :, 0:n], s, spread_in(smax[0:n, :], [n, QUART, n]),
                                ALU.subtract).then_inc(S["diff_done"], 1)

            def dve_token(G):
                n = G.n
                dve.wait_ge(S["tok_done"], G.g + 1)
                wait(dve, S["base_done"], G.g)
                V.tensor_tensor(tok[0:n, :], bank[5][0:n, 0:D], b2r[0:n, :], ALU.add).then_inc(S["ln1_stat"], 1)
                wait_alone(dve, S["ln1_stat"], G.g * 3 + 1)
                V.bn_stats(stat[0:n, 0, :], tok[0:n, :]).then_inc(S["ln1_stat"], 1)
                wait_alone(dve, S["ln1_stat"], G.g * 3 + 2)
                V.bn_aggr(mv[0:n, 0, :], stat[0:n, 0:1, :]).then_inc(S["ln1_stat"], 1)

            def dve_norm1(G):
                n = G.n
                dve.wait_ge(S["ln1_rstd"], G.g * 2 + 2)
                wait(dve, S["t1_done"], G.g)
                V.tensor_scalar(xn[0:n, :], tok[0:n, :], mv[0:n, 0, 0:1], rstd[0:n, 0, :], ALU.subtract,
                                ALU.mult).then_inc(S["ln1_done"], 1)

            def dve_residual(G):
                n = G.n
                r = resid[0:n, ds(G.g * D, D)]
                dve.wait_ge(S["o_done"], G.g + 1)
                dve.wait_ge(S["base_done"], G.g + 1)
                V.tensor_tensor(r, bank[7][0:n, 0:D], r, ALU.add).then_inc(S["x1_done"], 1)
                wait_alone(dve, S["x1_done"], G.g + 1)
                V.bn_stats(stat[0:n, 1, :], r).then_inc(S["ln2_stat"], 1)
                wait_alone(dve, S["ln2_stat"], G.g * 2 + 1)
                V.bn_aggr(mv[0:n, 1, :], stat[0:n, 1:2, :]).then_inc(S["ln2_stat"], 1)

            def dve_norm2(G):
                n = G.n
                dve.wait_ge(S["ln2_rstd"], G.g * 2 + 2)
                wait(dve, S["t3_done"], G.g)
                wait(dve, S["routed_ready"], G.g)
                V.tensor_scalar(xn2[0:n, :], resid[0:n, ds(G.g * D, D)], mv[0:n, 1, 0:1], rstd[0:n, 1, :],
                                ALU.subtract, ALU.mult).then_inc(S["ln2_done"], 1)

            def dve_attention(G):
                n = G.n
                dve.wait_ge(S["pv_done"], G.g + 1)
                o = bank[7][0:n, 0:H * (DH + 1)].rearrange("p (h d) -> p h d", d=DH + 1)
                V.reciprocal(rsum[0:n, :, :], o[:, :, DH:DH + 1]).then_inc(S["rsum_done"], 1)
                dve.wait_ge(S["rsum_done"], G.g + 1)
                wait(dve, S["t2_done"], G.g)
                V.tensor_tensor(att[0:n, :].rearrange("p (h d) -> p h d", d=DH), o[:, :, 0:DH],
                                rsum[0:n, :, :].broadcast_to([n, H, DH]), ALU.mult).then_inc(S["att_done"], 1)

            def dve_values(G):
                n = G.n
                dve.wait_ge(S["v_done"], G.g + 1)
                V.tensor_tensor(v_ext[G.par][0:n, :, 0:DH], bank[5][0:n, 0:D].rearrange("p (h d) -> p h d", d=DH),
                                vbr[0:n, :].rearrange("p (h d) -> p h d", d=DH), ALU.add).then_inc(S["v_ready"], 1)

            def step_a(at):
                new, mid, old = at(0), at(1), at(2)
                if new.exists:
                    dve_silu(new)
                if mid.exists:
                    softmax(mid, 0)
                    softmax(mid, 1)
                    softmax(mid, 2)
                if new.exists:
                    dve_token(new)
                if mid.exists:
                    softmax(mid, 3)
                if new.exists:
                    dve_norm1(new)
                if old.exists:
                    dve_residual(old)
                if mid.exists:
                    dve_attention(mid)
                if old.exists:
                    dve_norm2(old)
                if new.exists:
                    dve_values(new)

            dve.wait_ge(S["cols_in"], 16)
            dve.wait_ge(S["rows_in"], 16)
            pipeline(dve, step_a, 2)

            def choose(G):
                n = G.n
                r, base = S["route"], G.g * ROUTE
                dve.wait_ge(S["logit_done"], G.g + 1)
                V.tensor_tensor(logit[0:n, :], bank[2][0:n, 0:E], gb2r[0:n, :], ALU.add).then_inc(r, 1)
                wait_alone(dve, r, base + 1)
                V.max(top[0:n, :], logit[0:n, :]).then_inc(r, 1)
                wait_alone(dve, r, base + 2)
                V.max_index(topi[0:n, :], top[0:n, :], logit[0:n, :]).then_inc(r, 1)
                dve.wait_ge(r, base + 3)
                V.tensor_copy(topf[0:n, :], topi[0:n, 0:2]).then_inc(r, 1)
                dve.wait_ge(r, base + 4)
                for k in range(2):
                    V.tensor_scalar(hot[G.par][0:n, k, :], const[0:n, C_IOTA:C_IOTA + E], topf[0:n, k:k + 1], None,
                                    ALU.is_equal).then_inc(r, 1)
                dve.wait_ge(r, base + 6)
                wait(dve, S["rank_done"], G.g - 1)
                V.tensor_tensor(chosen[G.par][0:n, :], hot[G.par][0:n, 0, :], hot[G.par][0:n, 1, :],
                                ALU.add).then_inc(r, 1)
                dve.wait_ge(r, base + 7)
                wait(dve, S["rank_done"], G.g)
                nxt, cur = before[(G.r + 1) % 2], before[G.par]
                if n < NG:
                    V.tensor_copy(nxt[:, :], cur[:, :]).then_inc(S["before_set"], 1)
                    dve.wait_ge(S["before_set"], 2)
                V.tensor_tensor(nxt[0:n, :], cur[0:n, :], chosen[G.par][0:n, :], ALU.add).then_inc(r, 1)
                V.tensor_scalar(gap[0:n, :], top[0:n, :], top[0:n, 0:1], None, ALU.subtract).then_inc(r, 1)

            def gate(G):
                n = G.n
                r, base = S["route"], G.g * ROUTE
                dve.wait_ge(S["htanh_done"], G.g + 1)
                V.tensor_scalar(num[0:n, :], half_tanh[0:n, :], 1.0, None, ALU.add).then_inc(r, 1)
                V.tensor_scalar(den[0:n, :], half_tanh[0:n, :], -1.0, 1.0, ALU.mult, ALU.add).then_inc(r, 1)
                dve.wait_ge(r, base + 11)
                V.reciprocal(den[0:n, :], den[0:n, :]).then_inc(r, 1)
                dve.wait_ge(r, base + 12)
                V.scalar_tensor_tensor(out=num[0:n, :], in0=num[0:n, :], scalar=1.0, in1=den[0:n, :], op0=ALU.mult,
                                       op1=ALU.mult, accum_out=gsum[0:n, :]).then_inc(r, 1)
                dve.wait_ge(r, base + 13)
                V.reciprocal(gsum[0:n, :], gsum[0:n, :]).then_inc(r, 1)
                dve.wait_ge(r, base + 14)
                wait(dve, S["sent_ready"], G.g - 1)
                V.tensor_scalar(gates[G.par][0:n, :], num[0:n, 0:2], gsum[0:n, :], None, ALU.mult).then_inc(r, 1)

            def slots(G):
                n = G.n
                r, base = S["slot_steps"], G.g * SLOT
                dve.wait_ge(S["rank_done"], G.g + 1)
                V.tensor_tensor(slot_of[0:n, :], bank[3][0:n, 0:E], const[0:n, C_BASE:C_BASE + E],
                                ALU.add).then_inc(r, 1)
                dve.wait_ge(r, base + 1)
                V.tensor_tensor(slot_tmp[0:n, :, :], hot[G.par][0:n, :, :], spread(slot_of[0:n, :], [n, 2, E]),
                                ALU.mult).then_inc(r, 1)
                dve.wait_ge(r, base + 2)
                V.reduce_sum(slot_f[0:n, :], slot_tmp[0:n, :, :], AX.X).then_inc(r, 1)
                dve.wait_ge(r, base + 3)
                wait(dve, S[f"scatter{G.par}"], (G.use(2) - 1) * 32)
                V.tensor_copy(slot_i[G.par][0:n, :], slot_f[0:n, :]).then_inc(r, 1)

            def step_b(at):
                if at(1).exists:
                    choose(at(1))
                if at(2).exists:
                    slots(at(2))
                if at(1).exists:
                    gate(at(1))

            pipeline(dve, step_b, 2)

            st = S["table_steps"]
            done = [0]

            def then(instruction):
                done[0] += 1
                instruction.then_inc(st, 1)
                dve.wait_ge(st, done[0])

            def by_expert(x):
                return spread(x, [1, TILES, E])

            dve.wait_ge(S["totals_done"], 1)
            then(V.tensor_copy(counts, bank[3][0:1, 0:E]))
            then(V.tensor_copy(count_i[:, 0:E], counts))
            then(V.tensor_scalar(wt, counts, float(P - 1), None, ALU.add))
            then(V.tensor_copy(count_i[:, E:2 * E], wt))
            then(V.tensor_scalar(count_i[:, E:2 * E], count_i[:, E:2 * E], 7, None, ALU.logical_shift_right))
            then(V.tensor_copy(ntile, count_i[:, E:2 * E]))
            ltv = lt_tmp[:, :].rearrange("p (a b) -> p a b", b=E)
            then(V.tensor_tensor(ltv, const[0:1, C_LT:C_LT + E * E].rearrange("p (a b) -> p a b", b=E),
                                 spread(ntile, [1, E, E]), ALU.mult))
            then(V.reduce_sum(start_t, ltv, AX.X))
            then(V.tensor_tensor(end_t, start_t, ntile, ALU.add))
            then(V.scalar_tensor_tensor(out=wt, in0=start_t, scalar=-float(P), in1=const[0:1, C_BASE:C_BASE + E],
                                        op0=ALU.mult, op1=ALU.add))
            jv = const[0:1, C_J:C_J + TILES * E].rearrange("p (j e) -> p j e", e=E)
            then(V.tensor_tensor(tb[0], jv, by_expert(start_t), ALU.is_ge))
            then(V.tensor_tensor(tb[1], jv, by_expert(end_t), ALU.is_lt))
            then(V.tensor_tensor(tb[0], tb[0], tb[1], ALU.mult))
            then(V.scalar_tensor_tensor(out=tb[2], in0=jv, scalar=float(P), in1=by_expert(wt), op0=ALU.mult,
                                        op1=ALU.add))
            then(V.tensor_tensor(tb[3], tb[0], tb[2], ALU.mult))
            then(V.tensor_tensor(tb[4], tb[0], by_expert(const[0:1, C_IOTA:C_IOTA + E]), ALU.mult))
            then(V.reduce_sum(table_f[:, 0:TILES], tb[3], AX.X))
            then(V.reduce_sum(table_f[:, TILES:2 * TILES], tb[4], AX.X))
            then(V.reduce_sum(table_f[:, 2 * TILES:], tb[0], AX.X))
            then(V.tensor_scalar(table_f[:, 2 * TILES:], table_f[:, 2 * TILES:], -float(DUMMY), float(DUMMY),
                                 ALU.mult, ALU.add))
            then(V.tensor_tensor(table_f[:, 0:TILES], table_f[:, 0:TILES], table_f[:, 2 * TILES:], ALU.add))
            V.tensor_copy(table[:, :], table_f[:, 0:2 * TILES]).then_inc(S["tabled"], 1)

            def dve_shared(G):
                n = G.n
                r = resid[0:n, ds(G.g * D, D)]
                dve.wait_ge(S["so_done"], G.g + 1)
                V.tensor_tensor(r, bank[4 + G.par][0:n, 0:D], r, ALU.add).then_inc(S["acc_ready"], 1)

            def step_c(at):
                if at(1).exists:
                    dve_shared(at(1))

            dve.wait_ge(S["pool_steps"], GROUPS)
            pipeline(dve, step_c, 1)

            def expert_of(G):
                return dve.value_load(table[0:1, ds(G.g + TILES, 1)], min_val=0, max_val=E - 1)

            def dve_epre(G):
                e = expert_of(G)
                dve.wait_ge(S["eh_done"], G.g + 1)
                wait(dve, S["egelu_done"], G.g)
                V.tensor_tensor(epre[:, :], bank[2 + G.par][:, :], be1r[:, ds(e * HID, HID)], ALU.add).then_inc(
                    S["epre_done"], 1)

            def dve_eht(G):
                dve.wait_ge(S["eht_done"], G.g + 1)
                V.tensor_copy(ehid_t[G.par][:, :, :],
                              bank[4 + G.par][:, :].rearrange("p (c n) -> p c n", c=CH)).then_inc(S["eht_ready"], 1)

            def dve_ey(G):
                e = expert_of(G)
                x = xe[G.r]
                dve.wait_ge(S["ey_done"], G.g + 1)
                V.tensor_tensor(ey[:, :], bank[6 + G.par][:, 0:D], be2r[:, ds(e * D, D)], ALU.add).then_inc(
                    S["ey_steps"], 1)
                wait(dve, S["added"], (G.g - 1) * 16)
                V.tensor_copy(etok[G.par][:, :], x[:, D:D + 1]).then_inc(S["ey_steps"], 1)
                dve.wait_ge(S["ey_steps"], G.g * 3 + 1)
                V.tensor_scalar(eout[G.par][:, :], ey[:, :], x[:, D + 1:D + 2], None, ALU.mult).then_inc(
                    S["ey_steps"], 1)

            def step_d(at):
                if at(1).exists:
                    dve_epre(at(1))
                if at(3).exists:
                    dve_ey(at(3))
                if at(2).exists:
                    dve_eht(at(2))

            dve.wait_ge(S["late_in"], 48)
            pipeline(dve, step_d, 3, TILES, 4)

        @block.gpsimd
        def _(pool):
            G_ = nc.gpsimd
            G_.memset(expo[:], -0.5)
            G_.memset(before[0][:], 0.0)
            G_.memset(before[1][:], 0.0).then_inc(S["before_set"], 1)
            G_.memset(pad[:], 0.0).then_inc(S["prep_steps"], 1)
            pool.wait_ge(S["const_in"], 16)
            pool.wait_ge(S["prep_steps"], 1)
            G_.tensor_copy(pad[:, D:D + 1], const[:, C_PADT:C_PADT + 1]).then_inc(S["pad_set"], 1)
            pool.wait_ge(S["rows_in"], 16)

            def pool_rstd(G, i, stat_sem, steps, rstd_sem):
                n = G.n
                wait_alone(pool, S[stat_sem], (G.g + 1) * steps)
                G_.tensor_scalar(rstd[0:n, i, :], mv[0:n, i, 1:2], EPS, None, ALU.add).then_inc(S[rstd_sem], 1)
                pool.wait_ge(S[rstd_sem], G.g * 2 + 1)
                G_.tensor_tensor(rstd[0:n, i, :], rstd[0:n, i, :], expo[0:n, :], ALU.pow).then_inc(S[rstd_sem], 1)

            def pool_base(G):
                n = G.n
                G_.tensor_tensor(resid[0:n, ds(G.g * D, D)], tok[0:n, :], obr[0:n, :], ALU.add).then_inc(
                    S["base_done"], 1)

            def pool_keep(G):
                n = G.n
                r = resid[0:n, ds(G.g * D, D)]
                wait_alone(pool, S["ln2_done"], G.g + 1)
                G_.tensor_copy(routed[0:n, ds(G.g * D, D)], xn2[0:n, :]).then_inc(S["routed_ready"], 1)
                G_.tensor_tensor(r, r, bs2r[0:n, :], ALU.add).then_inc(S["pool_steps"], 1)

            def pool_keys(G):
                n = G.n
                pool.wait_ge(S["k_ready"], G.g + 1)
                for c in range(CD):
                    last = G_.tensor_tensor(km[G.par][:, c * HC:(c + 1) * HC, 0:n],
                                            spread(k_t[:, c, 0:n], [P, HC, n]),
                                            spread_in(const[:, C_HEAD:C_HEAD + HC], [P, HC, n]), ALU.mult)
                last.then_inc(S["km_ready"], 1)

            def step_a(at):
                new, old = at(0), at(2)
                if new.exists:
                    pool_rstd(new, 0, "ln1_stat", 3, "ln1_rstd")
                    pool_base(new)
                if old.exists:
                    pool_rstd(old, 1, "ln2_stat", 2, "ln2_rstd")
                    pool_keep(old)
                if new.exists:
                    pool_keys(new)

            pipeline(pool, step_a, 2)

            def send(G):
                n, u = G.n, G.use(2)
                wait_alone(pool, S[f"scatter{G.par}"], (u - 1) * 32)
                for k in range(2):
                    G_.tensor_copy(sent[k][G.par][0:n, 0:D], routed[0:n, ds(G.g * D, D)])
                    G_.tensor_copy(sent[k][G.par][0:n, D:D + 1], const[0:n, ds(G.g + C_TOK, 1)])
                wait_alone(pool, S["route"], (G.g + 1) * ROUTE)
                for k in range(2):
                    last = G_.tensor_copy(sent[k][G.par][0:n, D + 1:D + 2], gates[G.par][0:n, k:k + 1])
                last.then_inc(S["sent_ready"], 1)
                pool.wait_ge(S["sent_ready"], G.g + 1)
                wait_alone(pool, S["slot_steps"], (G.g + 1) * SLOT)
                for k in range(2):
                    G_.indirect_dma_start(
                        out=a["slots"], out_offset=bass.IndirectOffsetOnAxis(ap=slot_i[G.par][0:n, k:k + 1], axis=0),
                        in_=sent[k][G.par][0:n, :], in_offset=None).then_inc(S[f"scatter{G.par}"], 16)

            def step_b(at):
                if at(2).exists:
                    send(at(2))

            pool.wait_ge(S["routed_ready"], GROUPS)
            pipeline(pool, step_b, 2)

            def add_rows(G):
                pool.wait_ge(S["ey_steps"], (G.g + 1) * 3)
                wait_alone(pool, S["added"], G.g * 16)
                G_.indirect_dma_start(
                    out=a["acc"], out_offset=bass.IndirectOffsetOnAxis(ap=etok[G.par][:, 0:1], axis=0),
                    in_=eout[G.par][:, :], in_offset=None, compute_op=ALU.add).then_inc(S["added"], 16)

            def step_d(at):
                if at(3).exists:
                    add_rows(at(3))

            pool.wait_ge(S["acc_in"], 16 * (GROUPS + 1))
            pipeline(pool, step_d, 3, TILES, 4)
            pool.wait_ge(S["added"], 16 * TILES)


def constants():
    import numpy as np

    c = np.zeros((P, C_N), np.float32)
    q = np.arange(P)
    c[:, C_ID:C_ID + P] = np.eye(P)
    k = np.arange(NG)
    seen = (q[:, None] // SEQ == k[None] // SEQ) & (k[None] <= q[:, None])
    c[:, C_MASK:C_MASK + NG] = np.where(seen, 0.0, -1e30)
    c[:, C_HEAD:C_HEAD + HC] = q[:, None] // DH == np.arange(HC)[None]
    c[:, C_TRI:C_TRI + P] = q[:, None] < q[None]
    e = np.arange(E)
    c[:, C_IOTA:C_IOTA + E] = e
    c[:, C_BASE:C_BASE + E] = e * REGION
    c[:, C_LT:C_LT + E * E] = (e[None] < e[:, None]).reshape(-1)
    c[:, C_J:C_J + TILES * E] = np.repeat(np.arange(TILES), E)
    c[:, C_TOK:C_TOK + GROUPS] = np.arange(GROUPS)[None] * NG + q[:, None]
    c[:, C_PADT] = T + q
    return c


def kernel(**inputs):
    import numpy as np
    import concourse.bacc as bacc
    from concourse.bass_utils import run_bass_kernel_spmd

    x = {k.replace("L0_", ""): np.asarray(v) for k, v in inputs.items()}
    C, G, PS = 3, 6, 16

    def chunks(w):
        return np.ascontiguousarray(w.reshape(-1, P, w.shape[-1]).transpose(1, 0, 2))

    t = x["x"].reshape(IMAGES, C, G, PS, G, PS).transpose(1, 3, 5, 0, 2, 4).reshape(KP, P, T)
    full = (GROUPS - 1) * NG
    patch = t[:, :, :full].reshape(KP, P, GROUPS - 1, NG).transpose(2, 1, 0, 3).reshape((GROUPS - 1) * P, KP * NG)
    col = lambda v: v.reshape(-1, P).T
    arrays = {
        "patch": patch,
        "patch_last": t[:, :, full:].transpose(1, 0, 2).reshape(P, KP * NL),
        "const": constants(),
        "w1": chunks(x["tok_W1"]),
        "w2": chunks(x["tok_W2"]),
        "wqk": chunks(np.concatenate([x["attn_q_w"].T, x["attn_k_w"].T], axis=1)),
        "wv": chunks(x["attn_v_w"].T),
        "wo": chunks(x["attn_o_w"].T),
        "gw1": chunks(x["ffn_gw1"]),
        "gw2": chunks(x["ffn_gw2"]),
        "ws1": chunks(x["ffn_Ws1"]),
        "ws2": chunks(x["ffn_Ws2"]),
        "we1": x["ffn_We1"].reshape(E, CD, P, HID).transpose(2, 0, 1, 3).reshape(P, -1),
        "we2": x["ffn_We2"].reshape(E, CH, P, D).transpose(2, 0, 1, 3).reshape(P, -1),
        "be1": x["ffn_be1"].reshape(1, -1),
        "be2": x["ffn_be2"].reshape(1, -1),
        "cols": np.concatenate([col(x["tok_b1"]), col(x["attn_q_b"]), col(x["attn_k_b"]), col(x["ffn_gb1"]),
                                col(x["ffn_bs1"])], axis=1),
        "rows": np.concatenate([x["tok_b2"], x["attn_v_b"], x["attn_o_b"], x["ffn_bs2"], x["ffn_gb2"]])[None],
    }
    arrays = {f"in_{k}": np.ascontiguousarray(v) for k, v in arrays.items()}
    nc = bacc.Bacc("TRN2", target_bir_lowering=False, num_devices=1)
    a = {k[3:]: nc.dram_tensor(k, v.shape, F32, kind="ExternalInput").ap() for k, v in arrays.items()}
    a["slots"] = nc.dram_tensor("slots", [DUMMY + P, ROW], F32, kind="Internal").ap()
    a["acc"] = nc.dram_tensor("out_acc", [T + P, D], F32, kind="ExternalOutput").ap()
    vit_kernel(nc, a)
    got = run_bass_kernel_spmd(nc, [arrays], core_ids=[0]).results[0]["out_acc"]
    return got[:T].reshape(IMAGES, SEQ, D)
```

```python
import concourse.bass as bass
from concourse import mybir
from contextlib import ExitStack

F32 = mybir.dt.float32
BF16 = mybir.dt.bfloat16
I32 = mybir.dt.int32
U32 = mybir.dt.uint32
ALU = mybir.AluOpType
ACT = mybir.ActivationFunctionType
AX = mybir.AxisListType
ds = bass.ds

P = 128
IMAGES, SEQ = 64, 36
D = 256
CD = D // P
KP = 768 // P
H, DH = 16, 16
HC = H // CD
HID = 512
CH = HID // P
E = 8
T = IMAGES * SEQ
NG = 3 * SEQ
GROUPS = -(-IMAGES // 3)
NL = T - (GROUPS - 1) * NG
ROW = D + 1 + E
REGION = T + P
DUMMY = E * REGION
TILES = 2 * T // P + E - 1
EPS = 1e-5
QUART = 4

C_ID = 0
C_MASK = C_ID + P
C_HEAD = C_MASK + NG
C_TRI = C_HEAD + HC
C_IOTA = C_TRI + P
C_BASE = C_IOTA + E
C_LT = C_BASE + E
C_J = C_LT + E * E
C_TOK = C_J + TILES * E
C_PADT = C_TOK + GROUPS
C_VALID = C_PADT + 1
C_N = C_VALID + 1
CHOOSE = 5
ROUTE = 16
SENDS = 4
VGAP = P - DH


class Group:

    def __init__(self, turns, turn, r, count):
        self.turns, self.turn, self.r = turns, turn, r
        self.g = turn * turns + r
        self.par = r % 2
        known = isinstance(self.g, int)
        self.exists = not known or 0 <= self.g < count
        self.n = NL if known and self.g == GROUPS - 1 else NG

    def is_number(self, g):
        return isinstance(self.g, int) and self.g == g

    def use(self, slots):
        return self.turn * (self.turns // slots) + self.r // slots + 1


def wait(engine, semaphore, value):
    if isinstance(value, int) and value <= 0:
        return
    engine.wait_ge(semaphore, value)


def wait_alone(engine, semaphore, value):
    if isinstance(value, int) and value <= 0:
        return
    engine.wait_ge(semaphore, value)
    if not isinstance(value, int):
        engine.nop(nofuse=True)


def pipeline(engine, step, depth, count=GROUPS, turns=2):
    start = -(-(depth + 2) // turns) * turns
    stop = (count - 1) // turns * turns

    def run(turn, u):
        step(lambda s: Group(turns, turn + (u - s) // turns, (u - s) % turns, count))

    for t in range(start):
        run(t // turns, t % turns)
    with engine.Fori(start // turns, stop // turns) as turn:
        for u in range(turns):
            run(turn, u)
    for t in range(stop, count + depth):
        run(t // turns, t % turns)


def spread(ap, shape):
    return ap.unsqueeze(1).broadcast_to(shape)


def spread_in(ap, shape):
    return ap.unsqueeze(2).broadcast_to(shape)


def vit_kernel(nc, a):
    ctx = ExitStack()
    with ctx:
        def sb(name, shape, dt=F32):
            return ctx.enter_context(nc.sbuf_tensor(name, shape, dt))

        def sem(name):
            return ctx.enter_context(nc.semaphore(name))

        const = sb("const", [P, C_N])
        ident = const[:, C_ID:C_ID + P]
        tri = const[:, C_TRI:C_TRI + P]
        ident_bf = sb("ident_bf", [P, NG], BF16)
        mask_bf = sb("mask_bf", [P, NG], BF16)
        ones = sb("ones", [P, P])
        tokw = sb("tokw", [P, (KP + CD) * D])
        w1 = tokw[:, 0:KP * D].rearrange("p (k n) -> p k n", k=KP)
        w2 = tokw[:, KP * D:].rearrange("p (k n) -> p k n", k=CD)
        wqk = sb("wqk", [P, CD, 2 * D])
        wv = sb("wv", [P, CD, D])
        wo = sb("wo", [P, CD, D])
        gw1 = sb("gw1", [P, CD, HID])
        gw2 = sb("gw2", [P, CH, E])
        ws1 = sb("ws1", [P, CD, HID])
        ws2 = sb("ws2", [P, CH, D])
        cols = sb("cols", [P, CD + 2 * CD + 2 * CH + 1])
        b1c, qkbc = cols[:, 0:CD], cols[:, CD:3 * CD]
        gb1c, bs1c = cols[:, 3 * CD:3 * CD + CH], cols[:, 3 * CD + CH:3 * CD + 2 * CH]
        gb2c = cols[0:E, 3 * CD + 2 * CH:]
        rows = sb("rows", [P, 4 * D])
        b2r, vbr, obr, bs2r = (rows[:, i * D:(i + 1) * D] for i in range(4))
        we1 = sb("we1", [P, E * CD * HID])
        resid = sb("resid", [P, GROUPS * D])
        routed = sb("routed", [P, GROUPS * ROW])
        xn2t_all = sb("xn2t_all", [P, CD, T])
        expo = sb("expo", [P, 1])
        warm = sb("warm", [P, 1])

        arena = sb("arena", [P, E * CH * D + E * HID + E * D])
        we2 = arena[:, 0:E * CH * D]
        be1r = arena[:, E * CH * D:E * CH * D + E * HID]
        be2r = arena[:, E * CH * D + E * HID:]
        used = [0]

        def piece(*shape):
            n = 1
            for s in shape:
                n *= s
            v = arena[:, used[0]:used[0] + n]
            used[0] += n
            assert used[0] <= E * CH * D + E * HID + E * D
            names = "abc"[:len(shape)]
            if len(shape) == 1:
                return v
            return v.rearrange(f"p ({' '.join(names)}) -> p {' '.join(names)}",
                               **{names[i]: shape[i] for i in range(len(shape) - 1)})

        def pair(*shape):
            return [piece(*shape), piece(*shape)]

        km = pair(CD * HC, NG)
        prob = piece(H, NG)
        prob_t = piece(H, NG)
        diff = pair(QUART, NG)
        patch = pair(KP, NG)
        q_t = pair(CD, NG)
        v_wide = pair(VGAP + H * P)

        pre = sb("pre", [P, CD, NG])
        tanh_h = sb("tanh_h", [P, CD, NG])
        silu = sb("silu", [P, CD, NG])
        tok = sb("tok", [P, D])
        stat = sb("stat", [P, 2, 6])
        mv = sb("mv", [P, 2, 2])
        rstd = sb("rstd", [P, 2, 1])
        xn = sb("xn", [P, D])
        xn_t = sb("xn_t", [P, CD, NG])
        k_t = sb("k_t", [P, CD, NG])
        smax = sb("smax", [P, H])
        rsum = sb("rsum", [P, H])
        rsum_w = sb("rsum_w", [P, H, DH])
        rsum_t = sb("rsum_t", [P, CD, NG])
        att_t = sb("att_t", [P, CD, NG])
        xn2 = sb("xn2", [P, D])

        gh = [wqk[:, i, 0:CH * NG].rearrange("p (c n) -> p c n", c=CH) for i in range(2)]
        logit_t = [sb(f"logit_t{i}", [E, NG]) for i in range(2)]
        at_ = [E * CH * D]

        def batch(*shape):
            n = GROUPS
            for d in shape:
                n *= d
            v = arena[:, at_[0]:at_[0] + n]
            at_[0] += n
            if len(shape) == 1:
                return v.rearrange("p (g e) -> p g e", g=GROUPS)
            return v.rearrange("p (g k e) -> p g k e", g=GROUPS, k=shape[0])

        logit, order = sb("logit", [P, E]), sb("order", [P, E])
        whose = sb("whose", [P, E], U32)
        chosen = batch(E)
        before = [batch(E) for i in range(2)]
        place_of, num, den = batch(E), batch(E), batch(E)
        topf, hot, hot_place = batch(2), batch(2, E), batch(2, E)
        gsum = batch(1)
        assert at_[0] <= E * CH * D + E * HID
        slot_f = sb("slot_f", [P, GROUPS * 2])
        count_all = sb("count_all", [P, E])
        slot_now = [sb(f"slot_now{i}", [P, 2], U32) for i in range(SENDS)]
        sent = [sb(f"sent{i}", [P, ROW]) for i in range(SENDS)]
        pad = sb("pad", [P, ROW])

        tf = tokw[0:1, 0:8 * E + 5 * TILES * E]
        counts, ntile, start_t, end_t = (tf[:, i * E:(i + 1) * E] for i in range(4))
        wt = tf[:, 4 * E:5 * E]
        tb = [tf[:, 8 * E + i * TILES * E:8 * E + (i + 1) * TILES * E].rearrange("p (j e) -> p j e", e=E)
              for i in range(5)]
        table_f = sb("table_f", [1, 3 * TILES])
        table = sb("table", [1, 2 * TILES], I32)
        count_i = sb("count_i", [1, 2 * E], I32)
        lt_tmp = sb("lt_tmp", [1, E * E])

        left = [0]

        def late(*shape):
            n = shape[0] * (shape[1] if len(shape) > 1 else 1)
            v = routed[:, left[0]:left[0] + n]
            left[0] += n
            assert left[0] <= GROUPS * ROW
            return v if len(shape) == 1 else v.rearrange("p (c n) -> p c n", c=shape[0])

        xe = [late(ROW) for i in range(4)]
        xe_t = [late(CD, P) for i in range(2)]
        epre = late(HID)
        ehid = [late(HID) for i in range(2)]
        ehid_t = [late(CH, P) for i in range(2)]
        ey = late(D)
        eout = [late(D) for i in range(2)]
        etok = [sb(f"etok{i}", [P, 1], U32) for i in range(4)]
        egate = [sb(f"egate{i}", [P, 1]) for i in range(4)]

        bank = [ctx.enter_context(nc.psum_tensor(f"bank{i}", [P, 512], F32)) for i in range(8)]

        def view(b, c, n):
            return bank[b][:, 0:c * NG].rearrange("p (c n) -> p c n", n=NG)[:, :, 0:n]

        S = {name: sem(name) for name in """
            const_in w1_in w2_in wqk_in wv_in wo_in cols_in rows_in gw1_in gw2_in ws1_in ws2_in we1_in late_in
            patch0_in patch1_in prep_dve prep_steps v_zeroed pool_steps
            emb_done pre_done tanh_done silu_done tok_done ln1_stat ln1_rstd ln1_done base_done t1_done xnt_ready
            qk_done v_done q_ready k_ready km_ready v_ready score_done smax_done diff_done exp_done pt_done
            probt_ready pv_done rsum_done rt_done rt_ready attt_ready o_done x1_done ln2_stat ln2_rstd ln2_done
            t3_done xn2t_ready routed_ready
            gh_done gelu_done logit_done logit_out logitt_done choose route htanh_done rank_done
            scatter0 scatter1 scatter2 scatter3 sent_steps sent_ready totals_done table_steps tabled pad_set pads_in padacc_in
            sh_done shgelu_done so_done acc_ready acc_in
            xe0_in xe1_in xe2_in xe3_in xet_done xet_ready meta_done eh_done epre_done egelu_done eht_done eht_ready
            ey_done eyb_done eout_ready ey_steps added out_done
        """.split()}

        block = ctx.enter_context(nc.Block())

        @block.sync
        def _(sp):
            def load(dst, src, s, n=16):
                sp.dma_start(dst, src).then_inc(S[s], 16)

            load(w1, a["w1"], "w1_in")

            def load_patch(G):
                if not G.exists:
                    return
                wait(sp, S["emb_done"], G.g - 1)
                if G.n == NG:
                    src = a["patch"][ds(G.g * P, P), :]
                else:
                    src = a["patch_last"]
                dst = patch[G.par][:, :, 0:G.n]
                sp.dma_start(dst, src.rearrange("p (k n) -> p k n", k=KP)).then_inc(S[f"patch{G.par}_in"], 16)

            load_patch(Group(2, 0, 0, GROUPS))
            load(cols[:], a["cols"], "cols_in")
            load(const[:], a["const"], "const_in")
            load(w2, a["w2"], "w2_in")
            load(rows[:], a["rows"].broadcast_to([P, 4 * D]), "rows_in")
            load_patch(Group(2, 0, 1, GROUPS))
            load(wqk[:], a["wqk"], "wqk_in")
            load(wv[:], a["wv"], "wv_in")
            load(wo[:], a["wo"], "wo_in")

            def step(at):
                G = at(0)
                if isinstance(G.g, int) and G.g < 2:
                    return
                load_patch(G)

            pipeline(sp, step, 0)
            load(gw1[:], a["gw1"], "gw1_in")
            load(gw2[:], a["gw2"], "gw2_in")
            load(ws1[:], a["ws1"], "ws1_in")
            load(ws2[:], a["ws2"], "ws2_in")
            load(we1[:], a["we1"], "we1_in")
            sp.wait_ge(S["pv_done"], GROUPS)
            sp.wait_ge(S["rt_done"], GROUPS)
            load(we2, a["we2"], "late_in")
            sp.wait_ge(S["pad_set"], 1)
            sp.dma_start(a["slots"][DUMMY:DUMMY + P, :], pad[:]).then_inc(S["pads_in"], 16)
            sp.dma_start(a["acc"][T:T + P, :], pad[:, 0:D]).then_inc(S["acc_in"], 16)
            sp.wait_ge(S["tabled"], 1)
            for e in range(E):
                c = sp.value_load(count_i[0:1, e:e + 1], min_val=0, max_val=T)
                sp.dma_start(a["slots"][ds(c + e * REGION, P), :], pad[:]).then_inc(S["pads_in"], 16)
            sp.wait_ge(S["tabled"], 1)
            sp.wait_ge(S["sent_ready"], 1)
            load(be1r, a["be1"].broadcast_to([P, E * HID]), "late_in")
            load(be2r, a["be2"].broadcast_to([P, E * D]), "late_in")
            sp.wait_ge(S["pads_in"], 16 * (E + 1))
            for i in range(SENDS):
                sp.wait_ge(S[f"scatter{i}"], 16 * 2 * len(range(i, GROUPS, SENDS)))

            def tile_load(j, u):
                r = sp.value_load(table[0:1, ds(j, 1)], min_val=0, max_val=DUMMY)
                wait(sp, S["xet_done"], j - 3)
                wait(sp, S["meta_done"], j - 3)
                sp.dma_start(xe[u], a["slots"][ds(r, P), :]).then_inc(S[f"xe{u}_in"], 16)

            for j in range(4):
                tile_load(j, j)
            with sp.Fori(1, TILES // 4) as q:
                for u in range(4):
                    tile_load(q * 4 + u, u)
            for j in range(TILES // 4 * 4, TILES):
                tile_load(j, j % 4)
            sp.wait_ge(S["added"], 16 * TILES)

        @block.tensor
        def _(pe):
            mm = nc.tensor.matmul

            def embed(G):
                n = G.n
                if G.is_number(0):
                    pe.wait_ge(S["w1_in"], 16)
                pe.wait_ge(S[f"patch{G.par}_in"], 16 * G.use(2))
                wait(pe, S["rt_ready"], G.g - 1)
                for m in range(CD):
                    for k in range(KP):
                        last = mm(bank[4][:, m * NG:m * NG + n], w1[:, k, m * P:(m + 1) * P],
                                  patch[G.par][:, k, 0:n], start=k == 0, stop=k == KP - 1)
                last.then_inc(S["emb_done"], 1)

            def token(G):
                n = G.n
                if G.is_number(0):
                    pe.wait_ge(S["w2_in"], 16)
                    pe.wait_ge(S["prep_dve"], 1)
                pe.wait_ge(S["silu_done"], G.g + 1)
                wait(pe, S["v_ready"], G.g)
                for c in range(CD):
                    last = mm(bank[5][0:n, 0:D], silu[:, c, 0:n], w2[:, c, :], start=c == 0, stop=c == CD - 1)
                last.then_inc(S["tok_done"], 1)

            def norm1_t(G):
                n = G.n
                if G.is_number(0):
                    pe.wait_ge(S["const_in"], 16)
                pe.wait_ge(S["ln1_done"], G.g + 1)
                for c in range(CD):
                    last = nc.tensor.transpose(bank[4][:, c * NG:c * NG + n], xn[0:n, c * P:(c + 1) * P],
                                               ident[0:n, 0:n])
                last.then_inc(S["t1_done"], 1)

            def project_qk(b, first, n):
                for c in range(CD):
                    m = first + c
                    for k in range(CD):
                        last = mm(bank[b][:, c * NG:c * NG + n], wqk[:, k, m * P:(m + 1) * P], xn_t[:, k, 0:n],
                                  start=k == 0, stop=k == CD - 1)
                last.then_inc(S["qk_done"], 1)

            def qkv(new, mid):
                G = new
                n = G.n
                if G.is_number(0):
                    for s in "wqk_in wv_in".split():
                        pe.wait_ge(S[s], 16)
                pe.wait_ge(S["xnt_ready"], G.g + 1)
                wait(pe, S["k_ready"], G.g)
                wait(pe, S["xn2t_ready"], G.g - 1)
                project_qk(6, CD, n)
                if mid.exists:
                    sums_t(mid)
                for k in range(CD):
                    last = mm(bank[5][0:n, 0:D], xn_t[:, k, 0:n], wv[:, k, :], start=k == 0, stop=k == CD - 1)
                last.then_inc(S["v_done"], 1)
                wait(pe, S["probt_ready"], G.g * 4)
                project_qk(0, 0, n)

            def scores(G):
                n = G.n
                pe.wait_ge(S["q_ready"], G.g + 1)
                for j in range(H // QUART):
                    pe.wait_ge(S["km_ready"], G.g * CD + j * QUART // HC + 1)
                    wait(pe, S["probt_ready"], (G.g - 1) * 4 + j + 1)
                    o = view(j, QUART, n)[0:n]
                    c = j * QUART // HC
                    mm(o, q_t[G.par][:, c, 0:n], km[G.par][:, j * QUART:(j + 1) * QUART, 0:n], start=True, stop=False)
                    m = spread(mask_bf[0:n, 0:n], [n, QUART, n])
                    mm(o, ident_bf[0:n, 0:n], m, start=False, stop=True).then_inc(S["score_done"], 1)

            def probs_t(G, j):
                n = G.n
                pe.wait_ge(S["exp_done"], G.g * 4 + j + 1)
                for i in range(QUART):
                    last = nc.tensor.transpose(bank[j][0:n, i * NG:i * NG + n], prob[0:n, j * QUART + i, 0:n],
                                               ident[0:n, 0:n])
                last.then_inc(S["pt_done"], 1)

            def values(G, j):
                n = G.n
                pe.wait_ge(S["v_ready"], G.g + 1)
                wait(pe, S["attt_ready"], G.g)
                c = j * QUART // HC
                pe.wait_ge(S["probt_ready"], G.g * 4 + j + 1)
                for h in range(j * QUART, (j + 1) * QUART):
                    at = VGAP + h * P - DH * (h % HC)
                    last = mm(bank[7][:, c * NG:c * NG + n], v_wide[G.par][0:n, at:at + P], prob_t[0:n, h, 0:n],
                              start=h % HC == 0, stop=h % HC == HC - 1)
                if h == H - 1:
                    last.then_inc(S["pv_done"], 1)

            def sums_t(G):
                n = G.n
                pe.wait_ge(S["rsum_done"], G.g * 3 + 3)
                nxt = min(G.g + 2, GROUPS) if isinstance(G.g, int) else G.g + 2
                pe.wait_ge(S["xnt_ready"], nxt)
                for c in range(CD):
                    last = nc.tensor.transpose(bank[4][:, (CD + c) * NG:(CD + c) * NG + n],
                                               rsum_w[0:n, c * HC:(c + 1) * HC, :].rearrange("p h d -> p (h d)"),
                                               ident[0:n, 0:n])
                last.then_inc(S["rt_done"], 1)

            def project(G):
                n = G.n
                if G.is_number(0):
                    pe.wait_ge(S["wo_in"], 16)
                pe.wait_ge(S["attt_ready"], G.g + 1)
                nxt = min(G.g + 2, GROUPS) if isinstance(G.g, int) else G.g + 2
                pe.wait_ge(S["k_ready"], nxt)
                wait(pe, S["xn2t_ready"], G.g)
                for c in range(CD):
                    last = mm(bank[6][0:n, 0:D], att_t[:, c, 0:n], wo[:, c, :], start=c == 0, stop=c == CD - 1)
                last.then_inc(S["o_done"], 1)

            def norm2_t(G):
                n = G.n
                pe.wait_ge(S["ln2_done"], G.g + 1)
                for c in range(CD):
                    last = nc.tensor.transpose(bank[6][:, c * NG:c * NG + n], xn2[0:n, c * P:(c + 1) * P],
                                               ident[0:n, 0:n])
                last.then_inc(S["t3_done"], 1)

            def step_a(at):
                new, mid, old = at(0), at(1), at(2)
                if new.exists:
                    embed(new)
                if mid.exists:
                    scores(mid)
                if new.exists:
                    token(new)
                if old.exists:
                    project(old)
                if mid.exists:
                    probs_t(mid, 0)
                    probs_t(mid, 1)
                    probs_t(mid, 2)
                    values(mid, 0)
                    probs_t(mid, 3)
                    values(mid, 1)
                    values(mid, 2)
                if new.exists:
                    norm1_t(new)
                if old.exists:
                    norm2_t(old)
                if mid.exists:
                    values(mid, 3)
                if new.exists:
                    qkv(new, mid)
                elif mid.exists:
                    sums_t(mid)

            pipeline(pe, step_a, 2)

            def route_hidden(G):
                n = G.n
                wait(pe, S["gelu_done"], G.g - 1)
                for m in range(CH):
                    for k in range(CD):
                        last = mm(bank[G.par][:, m * NG:m * NG + n], gw1[:, k, m * P:(m + 1) * P],
                                  xn2t_all[:, k, ds(G.g * NG, n)], start=k == 0, stop=k == CD - 1)
                last.then_inc(S["gh_done"], 1)

            def route_logits(G):
                n = G.n
                pe.wait_ge(S["gelu_done"], G.g + 1)
                wait(pe, S["logit_out"], G.g - 1)
                for c in range(CH):
                    last = mm(bank[2 + G.par][0:E, 0:n], gw2[:, c, :], gh[G.par][:, c, 0:n], start=c == 0,
                              stop=c == CH - 1)
                last.then_inc(S["logit_done"], 1)

            def logits_t(G):
                n = G.n
                wait(pe, S["choose"], (G.g - 2) * CHOOSE + 1)
                wait_alone(pe, S["logit_out"], G.g + 1)
                nc.tensor.transpose(bank[4 + G.par][0:n, 0:E], logit_t[G.par][:, 0:n], ident[0:E, 0:E]).then_inc(
                    S["logitt_done"], 1)

            def step_b(at):
                new, mid, old = at(0), at(1), at(2)
                if new.exists:
                    route_hidden(new)
                if mid.exists:
                    route_logits(mid)
                if old.exists:
                    logits_t(old)

            pe.wait_ge(S["gw1_in"], 16)
            pe.wait_ge(S["gw2_in"], 16)
            pe.wait_ge(S["xn2t_ready"], GROUPS)
            pe.wait_ge(S["probt_ready"], 4 * GROUPS)
            pipeline(pe, step_b, 2)
            def rank():
                pe.wait_ge(S["route"], 10)
                ranks = bank[6][0:NG, 0:GROUPS * E]
                mm(ranks, tri[0:NG, 0:NG], chosen[0:NG].rearrange("p g e -> p (g e)"), start=True, stop=False)
                mm(ranks, ones[0:NG, 0:NG], before[1][0:NG].rearrange("p g e -> p (g e)"), start=False,
                   stop=True).then_inc(S["rank_done"], 1)
                mm(bank[7][0:1, 0:E], ones[0:NG, 0:1], count_all[0:NG, :], start=True, stop=True).then_inc(
                    S["totals_done"], 1)

            def shared_hidden(G):
                n = G.n
                wait(pe, S["shgelu_done"], G.g - 1)
                for m in range(CH):
                    for k in range(CD):
                        last = mm(bank[G.par][:, m * NG:m * NG + n], ws1[:, k, m * P:(m + 1) * P],
                                  xn2t_all[:, k, ds(G.g * NG, n)], start=k == 0, stop=k == CD - 1)
                last.then_inc(S["sh_done"], 1)

            def shared_out(G):
                n = G.n
                if G.is_number(0):
                    pe.wait_ge(S["choose"], CHOOSE * GROUPS)
                pe.wait_ge(S["shgelu_done"], G.g + 1)
                wait(pe, S["acc_ready"], G.g - 1)
                for c in range(CH):
                    last = mm(bank[4 + G.par][0:n, 0:D], gh[G.par][:, c, 0:n], ws2[:, c, :],
                              start=c == 0, stop=c == CH - 1)
                last.then_inc(S["so_done"], 1)

            def step_c(at):
                if at(0).exists:
                    shared_hidden(at(0))
                if at(1).exists:
                    shared_out(at(1))
                if at(0).is_number(2):
                    rank()

            pe.wait_ge(S["ws1_in"], 16)
            pe.wait_ge(S["ws2_in"], 16)
            pe.wait_ge(S["gelu_done"], GROUPS)
            pipeline(pe, step_c, 1)

            pe.wait_ge(S["tabled"], 1)
            pe.wait_ge(S["we1_in"], 16)
            pe.wait_ge(S["late_in"], 48)
            pe.wait_ge(S["shgelu_done"], GROUPS)
            pe.wait_ge(S["acc_ready"], GROUPS)

            def expert_of(G):
                return pe.value_load(table[0:1, ds(G.g + TILES, 1)], min_val=0, max_val=E - 1)

            def rows_t(G):
                u4 = G.r
                wait(pe, S["xet_ready"], G.g - 1)
                pe.wait_ge(S[f"xe{u4}_in"], 16 * G.use(4))
                for c in range(CD):
                    last = nc.tensor.transpose(bank[G.par][:, c * P:(c + 1) * P], xe[u4][:, c * P:(c + 1) * P],
                                               ident[:, :])
                last.then_inc(S["xet_done"], 1)

            def up(G):
                e = expert_of(G)
                pe.wait_ge(S["xet_ready"], G.g + 1)
                wait(pe, S["epre_done"], G.g - 1)
                for k in range(CD):
                    last = mm(bank[2 + G.par][:, :], xe_t[G.par][:, k, :], we1[:, ds(e * (CD * HID) + k * HID, HID)],
                              start=k == 0, stop=k == CD - 1)
                last.then_inc(S["eh_done"], 1)

            def hidden_t(G):
                pe.wait_ge(S["egelu_done"], G.g + 1)
                wait(pe, S["eht_ready"], G.g - 1)
                for c in range(CH):
                    last = nc.tensor.transpose(bank[4 + G.par][:, c * P:(c + 1) * P], ehid[G.par][:, c * P:(c + 1) * P],
                                               ident[:, :])
                last.then_inc(S["eht_done"], 1)

            def down(G):
                e = expert_of(G)
                pe.wait_ge(S["eht_ready"], G.g + 1)
                wait(pe, S["ey_steps"], (G.g - 2) * 2 + 1)
                for c in range(CH):
                    last = mm(bank[6 + G.par][:, 0:D], ehid_t[G.par][:, c, :], we2[:, ds(e * (CH * D) + c * D, D)],
                              start=c == 0, stop=c == CH - 1)
                last.then_inc(S["ey_done"], 1)

            def step_d(at):
                if at(1).exists:
                    up(at(1))
                if at(0).exists:
                    rows_t(at(0))
                if at(3).exists:
                    down(at(3))
                if at(2).exists:
                    hidden_t(at(2))

            pipeline(pe, step_d, 3, TILES, 4)

        @block.scalar
        def _(act):
            def act_tanh(G):
                wait(act, S["silu_done"], G.g)
                act.wait_ge(S["pre_done"], G.g + 1)
                nc.scalar.activation(tanh_h[:, :, 0:G.n], pre[:, :, 0:G.n], ACT.Tanh, scale=0.5).then_inc(
                    S["tanh_done"], 1)

            def act_rt(G):
                act.wait_ge(S["rt_done"], G.g + 1)
                nc.scalar.copy(rsum_t[:, :, 0:G.n], view(4, 2 * CD, G.n)[:, CD:, :]).then_inc(S["rt_ready"], 1)

            def act_exp(G, j):
                n = G.n
                act.wait_ge(S["diff_done"], G.g * 4 + j + 1)
                wait(act, S["pt_done"], (G.g - 1) * 4 + j + 1)
                wait(act, S["rsum_done"], (G.g - 1) * 3 + 1)
                nc.scalar.activation(prob[0:n, j * QUART:(j + 1) * QUART, 0:n], diff[j % 2][0:n, :, 0:n], ACT.Exp,
                                     scale=DH ** -0.5).then_inc(S["exp_done"], 1)

            def act_probt(G, j):
                n = G.n
                act.wait_ge(S["pt_done"], G.g * 4 + j + 1)
                wait(act, S["pv_done"], G.g)
                nc.scalar.copy(prob_t[0:n, j * QUART:(j + 1) * QUART, 0:n], view(j, QUART, n)[0:n]).then_inc(
                    S["probt_ready"], 1)

            def act_xnt(G):
                act.wait_ge(S["t1_done"], G.g + 1)
                nc.scalar.copy(xn_t[:, :, 0:G.n], view(4, CD, G.n)).then_inc(S["xnt_ready"], 1)

            def act_xn2t(G):
                act.wait_ge(S["t3_done"], G.g + 1)
                nc.scalar.copy(xn2t_all[:, :, ds(G.g * NG, G.n)], view(6, CD, G.n)).then_inc(S["xn2t_ready"], 1)

            def act_qk(G, i, dst, b):
                n = G.n
                act.wait_ge(S["qk_done"], G.g * 2 + i + 1)
                for c in range(CD):
                    m = (1 - i) * CD + c
                    last = nc.scalar.activation(dst[:, c, 0:n], bank[b][:, c * NG:c * NG + n], ACT.Identity,
                                                bias=qkbc[:, m:m + 1])
                last.then_inc(S["q_ready" if i else "k_ready"], 1)

            def step_a(at):
                new, mid, old = at(0), at(1), at(2)
                if new.exists:
                    act_tanh(new)
                if mid.exists:
                    act_exp(mid, 0)
                    act_exp(mid, 1)
                    act_exp(mid, 2)
                    act_probt(mid, 0)
                    act_exp(mid, 3)
                    act_probt(mid, 1)
                    act_probt(mid, 2)
                    act_probt(mid, 3)
                if new.exists:
                    act_xnt(new)
                if old.exists:
                    act_xn2t(old)
                if new.exists:
                    wait(act, S["km_ready"], new.g * CD)
                    act_qk(new, 0, k_t, 6)
                if mid.exists:
                    act_rt(mid)
                if new.exists:
                    act_qk(new, 1, q_t[new.par], 0)

            act.wait_ge(S["cols_in"], 16)
            nc.scalar.activation(warm[:], cols[:, 0:1], ACT.Tanh)
            pipeline(act, step_a, 2)

            def act_gelu(G):
                n = G.n
                act.wait_ge(S["gh_done"], G.g + 1)
                wait(act, S["logit_done"], G.g - 1)
                for m in range(CH):
                    last = nc.scalar.activation(gh[G.par][:, m, 0:n], bank[G.par][:, m * NG:m * NG + n], ACT.Gelu,
                                                bias=gb1c[:, m:m + 1])
                last.then_inc(S["gelu_done"], 1)

            def step_b(at):
                if at(0).exists:
                    act_gelu(at(0))

            pipeline(act, step_b, 2)
            act.wait_ge(S["choose"], CHOOSE * GROUPS)
            nc.scalar.activation(num[0:NG], num[0:NG], ACT.Tanh, scale=0.5).then_inc(S["htanh_done"], 1)

            def act_shared(G):
                n = G.n
                act.wait_ge(S["sh_done"], G.g + 1)
                act.wait_ge(S["logit_done"], GROUPS)
                wait(act, S["so_done"], G.g - 1)
                for m in range(CH):
                    last = nc.scalar.activation(gh[G.par][:, m, 0:n], bank[G.par][:, m * NG:m * NG + n],
                                                ACT.Gelu_apprx_tanh, bias=bs1c[:, m:m + 1])
                last.then_inc(S["shgelu_done"], 1)

            def acc_store(G):
                act.wait_ge(S["acc_ready"], G.g + 1)
                act.dma_start(a["acc"][ds(G.g * NG, G.n), :], resid[0:G.n, ds(G.g * D, D)]).then_inc(S["acc_in"], 16)

            def step_c(at):
                if at(0).exists:
                    act_shared(at(0))
                if at(2).exists:
                    acc_store(at(2))

            pipeline(act, step_c, 2)

            def act_rows(G):
                act.wait_ge(S["xet_done"], G.g + 1)
                nc.scalar.copy(xe_t[G.par][:, :, :], bank[G.par][:, 0:D].rearrange("p (c n) -> p c n", c=CD)).then_inc(
                    S["xet_ready"], 1)

            def act_egelu(G):
                act.wait_ge(S["epre_done"], G.g + 1)
                wait(act, S["eht_done"], G.g - 1)
                nc.scalar.activation(ehid[G.par][:, :], epre[:, :], ACT.Gelu_apprx_tanh).then_inc(S["egelu_done"], 1)

            def step_d(at):
                if at(0).exists:
                    act_rows(at(0))
                if at(1).exists:
                    act_egelu(at(1))

            pipeline(act, step_d, 3, TILES, 4)

        @block.vector
        def _(dve):
            V = nc.vector

            dve.wait_ge(S["const_in"], 16)
            V.tensor_copy(ident_bf[:], const[:, C_ID:C_ID + NG])
            V.tensor_copy(mask_bf[:], const[:, C_MASK:C_MASK + NG])
            dve.wait_ge(S["w2_in"], 16)
            V.tensor_scalar(w2, w2, 0.5, None, ALU.mult)
            V.memset(ones[:], 1.0).then_inc(S["prep_dve"], 1)

            def dve_pre(G):
                n = G.n
                dve.wait_ge(S["emb_done"], G.g + 1)
                wait(dve, S["silu_done"], G.g)
                for m in range(CD):
                    last = V.tensor_scalar(pre[:, m, 0:n], bank[4][:, m * NG:m * NG + n], b1c[:, m:m + 1], None,
                                           ALU.add)
                last.then_inc(S["pre_done"], 1)

            def dve_silu(G):
                n = G.n
                dve.wait_ge(S["tanh_done"], G.g + 1)
                wait(dve, S["tok_done"], G.g)
                V.scalar_tensor_tensor(out=silu[:, :, 0:n], in0=tanh_h[:, :, 0:n], scalar=1.0, in1=pre[:, :, 0:n],
                                       op0=ALU.add, op1=ALU.mult).then_inc(S["silu_done"], 1)

            def largest(G, j):
                n = G.n
                dve.wait_ge(S["score_done"], G.g * 4 + j + 1)
                wait(dve, S["diff_done"], (G.g - 1) * 4 + j + 1)
                V.reduce_max(smax[0:n, j * QUART:(j + 1) * QUART], view(j, QUART, n)[0:n], AX.X).then_inc(
                    S["smax_done"], 1)

            def below(G, j):
                n = G.n
                dve.wait_ge(S["smax_done"], G.g * 4 + j + 1)
                wait(dve, S["exp_done"], G.g * 4 + j - 1)
                V.tensor_tensor(diff[j % 2][0:n, :, 0:n], view(j, QUART, n)[0:n],
                                spread_in(smax[0:n, j * QUART:(j + 1) * QUART], [n, QUART, n]),
                                ALU.subtract).then_inc(S["diff_done"], 1)

            def dve_token(G):
                n = G.n
                dve.wait_ge(S["tok_done"], G.g + 1)
                wait(dve, S["base_done"], G.g)
                V.tensor_tensor(tok[0:n, :], bank[5][0:n, 0:D], b2r[0:n, :], ALU.add).then_inc(S["ln1_stat"], 1)
                wait_alone(dve, S["ln1_stat"], G.g * 3 + 1)
                V.bn_stats(stat[0:n, 0, :], tok[0:n, :]).then_inc(S["ln1_stat"], 1)
                wait_alone(dve, S["ln1_stat"], G.g * 3 + 2)
                V.bn_aggr(mv[0:n, 0, :], stat[0:n, 0:1, :]).then_inc(S["ln1_stat"], 1)

            def dve_norm1(G):
                n = G.n
                dve.wait_ge(S["ln1_rstd"], G.g * 2 + 2)
                wait(dve, S["t1_done"], G.g)
                V.tensor_scalar(xn[0:n, :], tok[0:n, :], mv[0:n, 0, 0:1], rstd[0:n, 0, :], ALU.subtract,
                                ALU.mult).then_inc(S["ln1_done"], 1)

            def dve_residual(G):
                n = G.n
                r = resid[0:n, ds(G.g * D, D)]
                dve.wait_ge(S["o_done"], G.g + 1)
                dve.wait_ge(S["base_done"], G.g + 1)
                V.tensor_tensor(r, bank[6][0:n, 0:D], r, ALU.add).then_inc(S["x1_done"], 1)
                wait_alone(dve, S["x1_done"], G.g + 1)
                V.bn_stats(stat[0:n, 1, :], r).then_inc(S["ln2_stat"], 1)
                wait_alone(dve, S["ln2_stat"], G.g * 2 + 1)
                V.bn_aggr(mv[0:n, 1, :], stat[0:n, 1:2, :]).then_inc(S["ln2_stat"], 1)

            def dve_norm2(G):
                n = G.n
                dve.wait_ge(S["ln2_rstd"], G.g * 2 + 2)
                wait(dve, S["t3_done"], G.g)
                wait(dve, S["routed_ready"], G.g)
                V.tensor_scalar(xn2[0:n, :], resid[0:n, ds(G.g * D, D)], mv[0:n, 1, 0:1], rstd[0:n, 1, :],
                                ALU.subtract, ALU.mult).then_inc(S["ln2_done"], 1)

            def dve_sums(G):
                n = G.n
                r = S["rsum_done"]
                dve.wait_ge(S["exp_done"], G.g * 4 + 4)
                V.reduce_sum(rsum[0:n, :], prob[0:n, :, 0:n], AX.X).then_inc(r, 1)
                dve.wait_ge(r, G.g * 3 + 1)
                V.reciprocal(rsum[0:n, :], rsum[0:n, :]).then_inc(r, 1)
                dve.wait_ge(r, G.g * 3 + 2)
                wait(dve, S["rt_done"], G.g)
                V.tensor_copy(rsum_w[0:n, :, :], spread_in(rsum[0:n, :], [n, H, DH])).then_inc(r, 1)

            def dve_attention(G):
                n = G.n
                dve.wait_ge(S["pv_done"], G.g + 1)
                dve.wait_ge(S["rt_ready"], G.g + 1)
                wait(dve, S["o_done"], G.g)
                V.tensor_tensor(att_t[:, :, 0:n], view(7, CD, n), rsum_t[:, :, 0:n], ALU.mult).then_inc(
                    S["attt_ready"], 1)

            def dve_values(G):
                n = G.n
                dve.wait_ge(S["v_done"], G.g + 1)
                dst = v_wide[G.par][0:n, VGAP:].rearrange("p (h d) -> p h d", d=P)[:, :, 0:DH]
                V.tensor_tensor(dst, bank[5][0:n, 0:D].rearrange("p (h d) -> p h d", d=DH),
                                vbr[0:n, :].rearrange("p (h d) -> p h d", d=DH), ALU.add).then_inc(S["v_ready"], 1)

            def step_a(at):
                new, mid, old = at(0), at(1), at(2)
                if new.exists:
                    dve_pre(new)
                if mid.exists:
                    largest(mid, 0)
                    largest(mid, 1)
                    below(mid, 0)
                if new.exists:
                    dve_silu(new)
                if mid.exists:
                    largest(mid, 2)
                    below(mid, 1)
                    largest(mid, 3)
                    below(mid, 2)
                    below(mid, 3)
                if new.exists:
                    dve_token(new)
                if old.exists:
                    dve_residual(old)
                if new.exists:
                    dve_norm1(new)
                if old.exists:
                    dve_norm2(old)
                if mid.exists:
                    dve_sums(mid)
                if mid.exists:
                    dve_attention(mid)
                if new.exists:
                    dve_values(new)

            dve.wait_ge(S["cols_in"], 16)
            dve.wait_ge(S["rows_in"], 16)
            dve.wait_ge(S["v_zeroed"], 1)
            pipeline(dve, step_a, 2)

            def dve_logits(G):
                wait(dve, S["logitt_done"], G.g - 1)
                dve.wait_ge(S["logit_done"], G.g + 1)
                V.tensor_scalar(logit_t[G.par][:, 0:G.n], bank[2 + G.par][0:E, 0:G.n], gb2c, None, ALU.add).then_inc(
                    S["logit_out"], 1)

            def choose(G):
                n = G.n
                r = S["choose"]
                dve.wait_ge(S["logitt_done"], G.g + 1)
                V.tensor_copy(logit[0:n, :], bank[4 + G.par][0:n, 0:E]).then_inc(r, 1)
                wait_alone(dve, r, G.g * CHOOSE + 1)
                V.max(order[0:n, :], logit[0:n, :]).then_inc(r, 1)
                wait_alone(dve, r, G.g * CHOOSE + 2)
                V.max_index(whose[0:n, :], order[0:n, :], logit[0:n, :]).then_inc(r, 1)
                V.tensor_scalar(of_group(num, E, G), logit[0:n, :], order[0:n, 0:1], None, ALU.subtract).then_inc(r, 1)
                dve.wait_ge(r, G.g * CHOOSE + 4)
                V.tensor_copy(of_group(topf, 2, G), whose[0:n, 0:2]).then_inc(r, 1)

            def of_group(x, width, G):
                return x[0:G.n].rearrange("p g e -> p (g e)")[:, ds(G.g * width, width)]

            def step_b(at):
                if at(1).exists:
                    dve_logits(at(1))
                if at(2).exists:
                    choose(at(2))

            dve.wait_ge(S["pv_done"], GROUPS)
            V.memset(num[:, GROUPS - 1, :], 0.0)
            V.memset(topf[:, GROUPS - 1, :], 0.0).then_inc(S["prep_dve"], 1)
            dve.wait_ge(S["prep_dve"], 2)
            pipeline(dve, step_b, 2)

            def dve_shared(G):
                n = G.n
                r = resid[0:n, ds(G.g * D, D)]
                dve.wait_ge(S["so_done"], G.g + 1)
                V.tensor_tensor(r, bank[4 + G.par][0:n, 0:D], r, ALU.add).then_inc(S["acc_ready"], 1)

            rt = S["route"]
            nth = [0]

            def after(instruction):
                nth[0] += 1
                instruction.then_inc(rt, 1)
                dve.wait_ge(rt, nth[0])

            dve.wait_ge(S["choose"], CHOOSE * GROUPS)
            a2 = lambda x: x[0:NG]
            four = [NG, GROUPS, 2, E]
            iota4 = const[0:NG, C_IOTA:C_IOTA + E].unsqueeze(1).unsqueeze(1).broadcast_to(four)
            after(V.tensor_tensor(a2(hot), iota4, a2(topf).unsqueeze(3).broadcast_to(four), ALU.is_equal))
            after(V.tensor_tensor(a2(chosen), a2(hot)[:, :, 0, :], a2(hot)[:, :, 1, :], ALU.add))
            after(V.tensor_scalar(a2(chosen)[:, GROUPS - 1, :], a2(chosen)[:, GROUPS - 1, :],
                                  const[0:NG, C_VALID:C_VALID + 1], None, ALU.mult))
            V.memset(before[0][:, 0:1, :], 0.0)
            after(V.tensor_copy(a2(before[0])[:, 1:, :], a2(chosen)[:, 0:GROUPS - 1, :]))
            for i in range(5):
                old, new, by = a2(before[i % 2]), a2(before[(i + 1) % 2]), 1 << i
                V.tensor_copy(new[:, 0:by, :], old[:, 0:by, :])
                after(V.tensor_tensor(new[:, by:, :], old[:, by:, :], old[:, 0:GROUPS - by, :], ALU.add))
            after(V.tensor_tensor(count_all[0:NG, :], a2(before[1])[:, GROUPS - 1, :], a2(chosen)[:, GROUPS - 1, :],
                                  ALU.add))
            dve.wait_ge(S["htanh_done"], 1)
            after(V.tensor_scalar(a2(den), a2(num), -1.0, 1.0, ALU.mult, ALU.add))
            after(V.reciprocal(a2(den), a2(den)))
            after(V.scalar_tensor_tensor(out=a2(num).rearrange("p g e -> p (g e)"),
                                         in0=a2(num).rearrange("p g e -> p (g e)"), scalar=1.0,
                                         in1=a2(den).rearrange("p g e -> p (g e)"), op0=ALU.add, op1=ALU.mult))
            after(V.reduce_sum(a2(gsum).rearrange("p g e -> p (g e)"), a2(num), AX.X))
            after(V.reciprocal(a2(gsum), a2(gsum)))
            rows_out = routed[0:NG, :].rearrange("p (g r) -> p g r", g=GROUPS)
            V.tensor_copy(rows_out[:, :, D:D + 1], const[0:NG, C_TOK:C_TOK + GROUPS].unsqueeze(2))
            after(V.tensor_tensor(rows_out[:, :, D + 1:], a2(num), a2(gsum).broadcast_to([NG, GROUPS, E]), ALU.mult))
            assert nth[0] == ROUTE, nth[0]

            dve.wait_ge(S["routed_ready"], GROUPS)
            dve.wait_ge(S["pool_steps"], GROUPS)
            for g in range(2):
                dve_shared(Group(2, 0, g, GROUPS))

            dve.wait_ge(S["rank_done"], 1)
            after(V.tensor_tensor(a2(place_of), bank[6][0:NG, 0:GROUPS * E].rearrange("p (g e) -> p g e", e=E),
                                  spread(const[0:NG, C_BASE:C_BASE + E], [NG, GROUPS, E]), ALU.add))
            after(V.tensor_tensor(a2(hot_place), a2(hot), a2(place_of).unsqueeze(2).broadcast_to(four), ALU.mult))
            after(V.reduce_sum(slot_f[0:NG, :], a2(hot_place).rearrange("p g k e -> p (g k) e"), AX.X))

            st = S["table_steps"]
            done = [0]

            def then(instruction):
                done[0] += 1
                instruction.then_inc(st, 1)
                dve.wait_ge(st, done[0])

            def by_expert(x):
                return spread(x, [1, TILES, E])

            def table_first():
                dve.wait_ge(S["totals_done"], 1)
                then(V.tensor_copy(counts, bank[7][0:1, 0:E]))
                then(V.tensor_copy(count_i[:, 0:E], counts))
                then(V.tensor_scalar(wt, counts, float(P - 1), None, ALU.add))
                then(V.tensor_copy(count_i[:, E:2 * E], wt))
                then(V.tensor_scalar(count_i[:, E:2 * E], count_i[:, E:2 * E], 7, None, ALU.logical_shift_right))
                then(V.tensor_copy(ntile, count_i[:, E:2 * E]))
                ltv = lt_tmp[:, :].rearrange("p (a b) -> p a b", b=E)
                then(V.tensor_tensor(ltv, const[0:1, C_LT:C_LT + E * E].rearrange("p (a b) -> p a b", b=E),
                                     spread(ntile, [1, E, E]), ALU.mult))
                then(V.reduce_sum(start_t, ltv, AX.X))
                then(V.tensor_tensor(end_t, start_t, ntile, ALU.add))
                then(V.scalar_tensor_tensor(out=wt, in0=start_t, scalar=-float(P), in1=const[0:1, C_BASE:C_BASE + E],
                                            op0=ALU.mult, op1=ALU.add))

            def table_rest():
                jv = const[0:1, C_J:C_J + TILES * E].rearrange("p (j e) -> p j e", e=E)
                then(V.tensor_tensor(tb[0], jv, by_expert(start_t), ALU.is_ge))
                then(V.tensor_tensor(tb[1], jv, by_expert(end_t), ALU.is_lt))
                then(V.tensor_tensor(tb[0], tb[0], tb[1], ALU.mult))
                then(V.scalar_tensor_tensor(out=tb[2], in0=jv, scalar=float(P), in1=by_expert(wt), op0=ALU.mult,
                                            op1=ALU.add))

            def table_sums():
                then(V.tensor_tensor(tb[3], tb[0], tb[2], ALU.mult))
                then(V.tensor_tensor(tb[4], tb[0], by_expert(const[0:1, C_IOTA:C_IOTA + E]), ALU.mult))
                then(V.reduce_sum(table_f[:, 0:TILES], tb[3], AX.X))
                then(V.reduce_sum(table_f[:, TILES:2 * TILES], tb[4], AX.X))

            def table_idle():
                then(V.reduce_sum(table_f[:, 2 * TILES:], tb[0], AX.X))
                then(V.tensor_scalar(table_f[:, 2 * TILES:], table_f[:, 2 * TILES:], -float(DUMMY), float(DUMMY),
                                     ALU.mult, ALU.add))
                then(V.tensor_tensor(table_f[:, 0:TILES], table_f[:, 0:TILES], table_f[:, 2 * TILES:], ALU.add))
                V.tensor_copy(table[:, :], table_f[:, 0:2 * TILES]).then_inc(S["tabled"], 1)

            def build(G):
                n = G.n
                wait(dve, S[f"scatter{G.r}"], (G.use(SENDS) - 1) * 32)
                V.tensor_copy(sent[G.r][0:n, :], routed[0:n, ds(G.g * ROW, ROW)])
                V.tensor_copy(slot_now[G.r][0:n, :], slot_f[0:n, ds(G.g * 2, 2)]).then_inc(S["sent_ready"], 1)

            def step_c(at):
                if at(3).exists and not (at(3).is_number(0) or at(3).is_number(1)):
                    dve_shared(at(3))
                if at(0).exists:
                    build(at(0))
                for g, table_part in enumerate((table_first, table_rest, table_sums, table_idle)):
                    if at(3).is_number(g + 1):
                        table_part()

            pipeline(dve, step_c, 6, GROUPS, SENDS)

            def expert_of(G):
                return dve.value_load(table[0:1, ds(G.g + TILES, 1)], min_val=0, max_val=E - 1)

            def dve_epre(G):
                e = expert_of(G)
                dve.wait_ge(S["eh_done"], G.g + 1)
                wait(dve, S["egelu_done"], G.g)
                V.tensor_tensor(epre[:, :], bank[2 + G.par][:, :], be1r[:, ds(e * HID, HID)], ALU.add).then_inc(
                    S["epre_done"], 1)
                dve.wait_ge(S[f"xe{G.r}_in"], 16 * G.use(4))
                wait(dve, S["added"], (G.g - 3) * 16)
                V.tensor_copy(etok[G.r][:, :], xe[G.r][:, D:D + 1])
                V.tensor_copy(egate[G.r][:, :], xe[G.r][:, ds(e + (D + 1), 1)]).then_inc(S["meta_done"], 1)

            def dve_eht(G):
                dve.wait_ge(S["eht_done"], G.g + 1)
                V.tensor_copy(ehid_t[G.par][:, :, :],
                              bank[4 + G.par][:, :].rearrange("p (c n) -> p c n", c=CH)).then_inc(S["eht_ready"], 1)

            def dve_ey(G):
                e = expert_of(G)
                dve.wait_ge(S["ey_done"], G.g + 1)
                dve.wait_ge(S["meta_done"], G.g + 1)
                V.tensor_tensor(ey[:, :], bank[6 + G.par][:, 0:D], be2r[:, ds(e * D, D)], ALU.add).then_inc(
                    S["ey_steps"], 1)
                wait(dve, S["added"], (G.g - 1) * 16)
                dve.wait_ge(S["ey_steps"], G.g * 2 + 1)
                V.tensor_scalar(eout[G.par][:, :], ey[:, :], egate[G.r][:, :], None, ALU.mult).then_inc(
                    S["ey_steps"], 1)

            def step_d(at):
                if at(3).exists:
                    dve_eht(at(3))
                if at(1).exists:
                    dve_epre(at(1))
                if at(3).exists:
                    dve_ey(at(3))

            dve.wait_ge(S["late_in"], 48)
            pipeline(dve, step_d, 3, TILES, 4)

        @block.gpsimd
        def _(pool):
            G_ = nc.gpsimd
            G_.memset(expo[:], -0.5)
            G_.memset(v_wide[0], 0.0)
            G_.memset(v_wide[1], 0.0).then_inc(S["v_zeroed"], 1)
            G_.memset(pad[:], 0.0).then_inc(S["prep_steps"], 1)
            pool.wait_ge(S["const_in"], 16)
            pool.wait_ge(S["prep_steps"], 1)
            G_.tensor_copy(pad[:, D:D + 1], const[:, C_PADT:C_PADT + 1]).then_inc(S["pad_set"], 1)
            pool.wait_ge(S["rows_in"], 16)

            def pool_rstd(G, i, stat_sem, steps, rstd_sem):
                n = G.n
                wait_alone(pool, S[stat_sem], (G.g + 1) * steps)
                G_.tensor_scalar(rstd[0:n, i, :], mv[0:n, i, 1:2], EPS, None, ALU.add).then_inc(S[rstd_sem], 1)
                pool.wait_ge(S[rstd_sem], G.g * 2 + 1)
                G_.tensor_tensor(rstd[0:n, i, :], rstd[0:n, i, :], expo[0:n, :], ALU.pow).then_inc(S[rstd_sem], 1)

            def pool_base(G):
                n = G.n
                G_.tensor_tensor(resid[0:n, ds(G.g * D, D)], tok[0:n, :], obr[0:n, :], ALU.add).then_inc(
                    S["base_done"], 1)

            def pool_keep(G):
                n = G.n
                r = resid[0:n, ds(G.g * D, D)]
                wait_alone(pool, S["ln2_done"], G.g + 1)
                G_.tensor_copy(routed[0:n, ds(G.g * ROW, D)], xn2[0:n, :]).then_inc(S["routed_ready"], 1)
                G_.tensor_tensor(r, r, bs2r[0:n, :], ALU.add).then_inc(S["pool_steps"], 1)

            def pool_keys(G):
                n = G.n
                pool.wait_ge(S["k_ready"], G.g + 1)
                for c in range(CD):
                    last = G_.tensor_tensor(km[G.par][:, c * HC:(c + 1) * HC, 0:n],
                                            spread(k_t[:, c, 0:n], [P, HC, n]),
                                            spread_in(const[:, C_HEAD:C_HEAD + HC], [P, HC, n]), ALU.mult)
                    last.then_inc(S["km_ready"], 1)

            def step_a(at):
                new, old = at(0), at(2)
                if new.exists:
                    pool_rstd(new, 0, "ln1_stat", 3, "ln1_rstd")
                if old.exists:
                    pool_rstd(old, 1, "ln2_stat", 2, "ln2_rstd")
                if new.exists:
                    pool_base(new)
                if old.exists:
                    pool_keep(old)
                if new.exists:
                    pool_keys(new)

            pipeline(pool, step_a, 2)

            def send(G):
                n = G.n
                wait_alone(pool, S["sent_ready"], G.g + 1)
                for k in range(2):
                    G_.indirect_dma_start(
                        out=a["slots"],
                        out_offset=bass.IndirectOffsetOnAxis(ap=slot_now[G.r][0:n, k:k + 1], axis=0),
                        in_=sent[G.r][0:n, :], in_offset=None).then_inc(S[f"scatter{G.r}"], 16)

            def step_c(at):
                if at(0).exists:
                    send(at(0))

            pipeline(pool, step_c, 1, GROUPS, SENDS)

            def add_rows(G):
                pool.wait_ge(S["ey_steps"], (G.g + 1) * 2)
                wait_alone(pool, S["added"], G.g * 16)
                G_.indirect_dma_start(
                    out=a["acc"], out_offset=bass.IndirectOffsetOnAxis(ap=etok[G.r][:, 0:1], axis=0),
                    in_=eout[G.par][:, :], in_offset=None, compute_op=ALU.add).then_inc(S["added"], 16)

            def step_d(at):
                if at(3).exists:
                    add_rows(at(3))

            pool.wait_ge(S["acc_in"], 16 * (GROUPS + 1))
            pipeline(pool, step_d, 3, TILES, 4)
            pool.wait_ge(S["added"], 16 * TILES)


def constants():
    import numpy as np

    c = np.zeros((P, C_N), np.float32)
    q = np.arange(P)
    c[:, C_ID:C_ID + P] = np.eye(P)
    k = np.arange(NG)
    seen = (q[:, None] // SEQ == k[None] // SEQ) & (k[None] <= q[:, None])
    c[:, C_MASK:C_MASK + NG] = np.where(seen, 0.0, -1e30)
    c[:, C_HEAD:C_HEAD + HC] = q[:, None] // DH == np.arange(HC)[None]
    c[:, C_TRI:C_TRI + P] = q[:, None] < q[None]
    e = np.arange(E)
    c[:, C_IOTA:C_IOTA + E] = e
    c[:, C_BASE:C_BASE + E] = e * REGION
    c[:, C_LT:C_LT + E * E] = (e[None] < e[:, None]).reshape(-1)
    c[:, C_J:C_J + TILES * E] = np.repeat(np.arange(TILES), E)
    c[:, C_TOK:C_TOK + GROUPS] = np.arange(GROUPS)[None] * NG + q[:, None]
    c[:, C_PADT] = T + q
    c[:, C_VALID] = q < NL
    return c


def kernel(**inputs):
    import numpy as np
    import concourse.bacc as bacc
    from concourse.bass_utils import run_bass_kernel_spmd

    x = {k.replace("L0_", ""): np.asarray(v) for k, v in inputs.items()}
    C, G, PS = 3, 6, 16

    def chunks(w):
        return np.ascontiguousarray(w.reshape(-1, P, w.shape[-1]).transpose(1, 0, 2))

    t = x["x"].reshape(IMAGES, C, G, PS, G, PS).transpose(1, 3, 5, 0, 2, 4).reshape(KP, P, T)
    full = (GROUPS - 1) * NG
    patch = t[:, :, :full].reshape(KP, P, GROUPS - 1, NG).transpose(2, 1, 0, 3).reshape((GROUPS - 1) * P, KP * NG)
    col = lambda v: v.reshape(-1, P).T
    arrays = {
        "patch": patch,
        "patch_last": t[:, :, full:].transpose(1, 0, 2).reshape(P, KP * NL),
        "const": constants(),
        "w1": chunks(x["tok_W1"]),
        "w2": chunks(x["tok_W2"]),
        "wqk": chunks(np.concatenate([x["attn_q_w"].T, x["attn_k_w"].T], axis=1)),
        "wv": chunks(x["attn_v_w"].T),
        "wo": chunks(x["attn_o_w"].T),
        "gw1": chunks(x["ffn_gw1"]),
        "gw2": chunks(x["ffn_gw2"]),
        "ws1": chunks(x["ffn_Ws1"]),
        "ws2": chunks(x["ffn_Ws2"]),
        "we1": x["ffn_We1"].reshape(E, CD, P, HID).transpose(2, 0, 1, 3).reshape(P, -1),
        "we2": x["ffn_We2"].reshape(E, CH, P, D).transpose(2, 0, 1, 3).reshape(P, -1),
        "be1": x["ffn_be1"].reshape(1, -1),
        "be2": x["ffn_be2"].reshape(1, -1),
        "cols": np.concatenate([col(x["tok_b1"]), col(x["attn_q_b"]), col(x["attn_k_b"]), col(x["ffn_gb1"]),
                                col(x["ffn_bs1"]), np.pad(x["ffn_gb2"], (0, P - E))[:, None]], axis=1),
        "rows": np.concatenate([x["tok_b2"], x["attn_v_b"], x["attn_o_b"], x["ffn_bs2"]])[None],
    }
    arrays = {f"in_{k}": np.ascontiguousarray(v) for k, v in arrays.items()}
    nc = bacc.Bacc("TRN2", target_bir_lowering=False, num_devices=1)
    a = {k[3:]: nc.dram_tensor(k, v.shape, F32, kind="ExternalInput").ap() for k, v in arrays.items()}
    a["slots"] = nc.dram_tensor("slots", [DUMMY + P, ROW], F32, kind="Internal").ap()
    a["acc"] = nc.dram_tensor("out_acc", [T + P, D], F32, kind="ExternalOutput").ap()
    vit_kernel(nc, a)
    got = run_bass_kernel_spmd(nc, [arrays], core_ids=[0]).results[0]["out_acc"]
    return got[:T].reshape(IMAGES, SEQ, D)
```

```python
import concourse.bass as bass
from concourse import mybir
from contextlib import ExitStack

F32 = mybir.dt.float32
I32 = mybir.dt.int32
U32 = mybir.dt.uint32
ALU = mybir.AluOpType
ACT = mybir.ActivationFunctionType
AX = mybir.AxisListType
ds = bass.ds

P = 128
IMAGES, SEQ = 64, 36
D = 256
CD = D // P
KP = 768 // P
H, DH = 16, 16
HC = H // CD
HID = 512
CH = HID // P
E = 8
T = IMAGES * SEQ
NG = 3 * SEQ
GROUPS = -(-IMAGES // 3)
NL = T - (GROUPS - 1) * NG
ROW = D + 1 + E
REGION = T + P
DUMMY = E * REGION
TILES = 2 * T // P + E - 1
EPS = 1e-5
QUART = 4

C_ID = 0
C_MASK = C_ID + P
C_HEAD = C_MASK + NG
C_TRI = C_HEAD + HC
C_IOTA = C_TRI + P
C_BASE = C_IOTA + E
C_LT = C_BASE + E
C_J = C_LT + E * E
C_TOK = C_J + TILES * E
C_PADT = C_TOK + GROUPS
C_VALID = C_PADT + 1
C_N = C_VALID + 1
CHOOSE = 5
DOUBLINGS = 5
COUNTED = 5 + DOUBLINGS
PAIRS = GROUPS // 2
SENDS = 4
BLOCK = 32
VSTEP = DH + BLOCK


class Group:

    def __init__(self, turns, turn, r, count):
        self.turns, self.turn, self.r = turns, turn, r
        self.g = turn * turns + r
        self.par = r % 2
        known = isinstance(self.g, int)
        self.exists = not known or 0 <= self.g < count
        self.n = NL if known and self.g == GROUPS - 1 else NG
        self.n2 = NG + NL if known and self.g == PAIRS - 1 else 2 * NG

    def group(self, i):
        return Group(2, self.g, i, GROUPS)

    def is_number(self, g):
        return isinstance(self.g, int) and self.g == g

    def use(self, slots):
        return self.turn * (self.turns // slots) + self.r // slots + 1


def wait(engine, semaphore, value):
    if isinstance(value, int) and value <= 0:
        return
    engine.wait_ge(semaphore, value)


def wait_alone(engine, semaphore, value):
    if isinstance(value, int) and value <= 0:
        return
    engine.wait_ge(semaphore, value)
    if not isinstance(value, int):
        engine.nop(nofuse=True)


def pipeline(engine, step, depth, count=GROUPS, turns=2, reach=0):
    start = -(-(depth + 2) // turns) * turns
    stop = (count - 1 - reach) // turns * turns

    def run(turn, u):
        step(lambda s: Group(turns, turn + (u - s) // turns, (u - s) % turns, count))

    for t in range(start):
        run(t // turns, t % turns)
    with engine.Fori(start // turns, stop // turns) as turn:
        for u in range(turns):
            run(turn, u)
    for t in range(stop, count + depth):
        run(t // turns, t % turns)


def ahead(G):
    number = G.g + 3
    if isinstance(number, int) and number >= CD * PAIRS:
        return None
    return number, G.turn + 1 + G.r, 1 - G.r


def silu_due(G):
    return G.exists and G.r == 1 and (not isinstance(G.turn, int) or G.turn + 1 < PAIRS)


def at_most(value, most):
    return min(value, most) if isinstance(value, int) else value


def head_at(i):
    c, s, b = i // HC, i // QUART % 2, i % QUART
    return c * HC + 2 * b + s


def spread(ap, shape):
    return ap.unsqueeze(1).broadcast_to(shape)


def spread_in(ap, shape):
    return ap.unsqueeze(2).broadcast_to(shape)


def vit_kernel(nc, a):
    ctx = ExitStack()
    with ctx:
        def sb(name, shape, dt=F32):
            return ctx.enter_context(nc.sbuf_tensor(name, shape, dt))

        def sem(name):
            return ctx.enter_context(nc.semaphore(name))

        const = sb("const", [P, C_N])
        ident = const[:, C_ID:C_ID + P]
        tri = const[:, C_TRI:C_TRI + P]
        ones = sb("ones", [P, P])
        tokw = sb("tokw", [P, (KP + CD) * D])
        w1 = tokw[:, 0:KP * D].rearrange("p (k n) -> p k n", k=KP)
        w2 = tokw[:, KP * D:].rearrange("p (k n) -> p k n", k=CD)
        wattn = sb("wattn", [P, CD * 4 * D])
        wqk = wattn[:, 0:CD * 2 * D].rearrange("p (k n) -> p k n", k=CD)
        wv = wattn[:, CD * 2 * D:CD * 3 * D].rearrange("p (k n) -> p k n", k=CD)
        wo = wattn[:, CD * 3 * D:].rearrange("p (k n) -> p k n", k=CD)
        gw1 = sb("gw1", [P, CD, HID])
        gw2 = sb("gw2", [P, CH, E])
        ws1 = sb("ws1", [P, CD, HID])
        ws2 = sb("ws2", [P, CH, D])
        cols = sb("cols", [P, CD + 2 * CD + 2 * CH + 1])
        b1c, qkbc = cols[:, 0:CD], cols[:, CD:3 * CD]
        gb1c, bs1c = cols[:, 3 * CD:3 * CD + CH], cols[:, 3 * CD + CH:3 * CD + 2 * CH]
        gb2c = cols[0:E, 3 * CD + 2 * CH:]
        rows = sb("rows", [P, 4 * D])
        b2r, vbr, obr, bs2r = (rows[:, i * D:(i + 1) * D] for i in range(4))
        we1 = sb("we1", [P, E * CD * HID])
        resid = sb("resid", [P, GROUPS * D])
        routed = sb("routed", [P, GROUPS * ROW])
        xn2t_all = sb("xn2t_all", [P, CD, T])
        expo = sb("expo", [P, 1])
        warm = sb("warm", [P, 1])

        arena = sb("arena", [P, E * CH * D + E * HID + E * D])
        we2 = arena[:, 0:E * CH * D]
        be1r = arena[:, E * CH * D:E * CH * D + E * HID]
        be2r = arena[:, E * CH * D + E * HID:]
        used = [0]

        def piece(*shape):
            n = 1
            for s in shape:
                n *= s
            v = arena[:, used[0]:used[0] + n]
            used[0] += n
            assert used[0] <= E * CH * D + E * HID + E * D
            names = "abc"[:len(shape)]
            if len(shape) == 1:
                return v
            return v.rearrange(f"p ({' '.join(names)}) -> p {' '.join(names)}",
                               **{names[i]: shape[i] for i in range(len(shape) - 1)})

        def pair(*shape):
            return [piece(*shape), piece(*shape)]

        km = pair(CD * HC, NG)
        prob = piece(H, NG)
        prob_t = piece(H, NG)
        patch = piece(KP, 2 * NG)
        q_t = pair(CD, NG)
        v_wide = pair(DH + H * VSTEP)

        pre = sb("pre", [P, CD, 2 * NG])
        tanh_h = sb("tanh_h", [P, CD, 2 * NG])
        silu = sb("silu", [P, CD, 2 * NG])
        tok = sb("tok", [P, D])
        stat = sb("stat", [P, 2, 6])
        mv = sb("mv", [P, 2, 2])
        rstd = sb("rstd", [P, 2, 1])
        xn = sb("xn", [P, D])
        xn_t = sb("xn_t", [P, CD, NG])
        k_t = sb("k_t", [P, CD, NG])
        smax = sb("smax", [P, H])
        rsum = sb("rsum", [P, H])
        rsum_w = sb("rsum_w", [P, H, DH])
        rsum_t = sb("rsum_t", [P, CD, NG])
        att_t = sb("att_t", [P, CD, NG])
        xn2 = sb("xn2", [P, D])

        gh = [wattn[:, i * CH * 2 * NG:(i + 1) * CH * 2 * NG].rearrange("p (c n) -> p c n", c=CH) for i in range(2)]
        at_ = [E * CH * D]

        def batch(*shape):
            n = GROUPS
            for d in shape:
                n *= d
            v = arena[:, at_[0]:at_[0] + n]
            at_[0] += n
            if len(shape) == 1:
                return v.rearrange("p (g e) -> p g e", g=GROUPS)
            return v.rearrange("p (g k e) -> p g k e", g=GROUPS, k=shape[0])

        logit, order = sb("logit", [P, E]), sb("order", [P, E])
        whose = sb("whose", [P, E], U32)
        chosen = batch(E)
        before = [batch(E) for i in range(2)]
        place_of, num = batch(E), batch(E)
        topf, hot, hot_place = batch(2), batch(2, E), batch(2, E)
        gsum = batch(1)
        logit_t = [arena[0:E, at_[0] + i * 2 * NG:at_[0] + (i + 1) * 2 * NG] for i in range(2)]
        at_[0] += 4 * NG
        assert at_[0] <= E * CH * D + E * HID
        slot_f = sb("slot_f", [P, GROUPS * 2])
        count_all = sb("count_all", [P, E])
        slot_now = [sb(f"slot_now{i}", [P, 2], U32) for i in range(SENDS)]
        sent = [sb(f"sent{i}", [P, ROW]) for i in range(SENDS)]
        pad = sb("pad", [P, ROW])

        tf = tokw[0:1, 0:8 * E + 5 * TILES * E]
        counts, ntile, start_t, end_t = (tf[:, i * E:(i + 1) * E] for i in range(4))
        wt = tf[:, 4 * E:5 * E]
        tb = [tf[:, 8 * E + i * TILES * E:8 * E + (i + 1) * TILES * E].rearrange("p (j e) -> p j e", e=E)
              for i in range(5)]
        table_f = sb("table_f", [1, 3 * TILES])
        table = sb("table", [1, 2 * TILES], I32)
        count_i = sb("count_i", [1, 2 * E], I32)
        lt_tmp = sb("lt_tmp", [1, E * E])

        left = [0]

        def late(*shape):
            n = shape[0] * (shape[1] if len(shape) > 1 else 1)
            v = routed[:, left[0]:left[0] + n]
            left[0] += n
            assert left[0] <= GROUPS * ROW
            return v if len(shape) == 1 else v.rearrange("p (c n) -> p c n", c=shape[0])

        xe = [late(ROW) for i in range(4)]
        xe_t = [late(CD, P) for i in range(2)]
        epre = late(HID)
        ehid = [late(HID) for i in range(2)]
        ehid_t = [late(CH, P) for i in range(2)]
        ey = late(D)
        eout = [late(D) for i in range(2)]
        etok = [sb(f"etok{i}", [P, 1], U32) for i in range(4)]
        egate = [sb(f"egate{i}", [P, 1]) for i in range(4)]

        bank = [ctx.enter_context(nc.psum_tensor(f"bank{i}", [P, 512], F32)) for i in range(8)]

        def view(b, c, n):
            return bank[b][:, 0:c * NG].rearrange("p (c n) -> p c n", n=NG)[:, :, 0:n]

        S = {name: sem(name) for name in """
            const_in w1_in w2_in wqk_in wv_in wo_in cols_in rows_in gw1_in gw2_in ws1_in ws2_in we1_in late_in
            patch_in prep_dve prep_steps v_zeroed pool_steps
            emb_done pre_done tanh_done silu_done tok_done ln1_stat ln1_rstd ln1_done base_done t1_done xnt_ready
            qk_done v_done q_ready k_ready km_ready v_ready score_done mask_done smax_done diff_done exp_done pt_done
            probt_ready pv_done rsum_done rt_done rt_ready attt_ready o_done x1_done ln2_stat ln2_rstd ln2_done
            t3_done xn2t_ready routed_ready
            gh_done gelu_done logit_done logit_out logitt_done choose route gate_exp_done rank_done
            scatter0 scatter1 scatter2 scatter3 sent_ready totals_done table_steps tabled pad_set pads_in
            sh_done shgelu_done so_done acc_ready acc_in
            xe0_in xe1_in xe2_in xe3_in xet_done xet_ready meta_done eh_done epre_done egelu_done eht_done eht_ready
            ey_done ey_steps added
        """.split()}

        block = ctx.enter_context(nc.Block())

        @block.sync
        def _(sp):
            def load(dst, src, s):
                sp.dma_start(dst, src).then_inc(S[s], 16)

            load(w1, a["w1"], "w1_in")

            def load_patch(i):
                wait(sp, S["emb_done"], i * CD)
                src = a["patch"][ds(i * P, P), :]
                sp.dma_start(patch, src.rearrange("p (k n) -> p k n", k=KP)).then_inc(S["patch_in"], 16)

            load_patch(0)
            load(cols[:], a["cols"], "cols_in")
            load(const[:], a["const"], "const_in")
            load(w2, a["w2"], "w2_in")
            load(rows[:], a["rows"].broadcast_to([P, 4 * D]), "rows_in")
            load(wqk, a["wqk"], "wqk_in")
            load(wv, a["wv"], "wv_in")
            load(wo, a["wo"], "wo_in")

            load_patch(1)
            with sp.Fori(2, PAIRS) as i:
                load_patch(i)
            load(gw1[:], a["gw1"], "gw1_in")
            load(gw2[:], a["gw2"], "gw2_in")
            load(ws1[:], a["ws1"], "ws1_in")
            load(ws2[:], a["ws2"], "ws2_in")
            load(we1[:], a["we1"], "we1_in")
            sp.wait_ge(S["pv_done"], GROUPS)
            sp.wait_ge(S["rt_done"], GROUPS)
            load(we2, a["we2"], "late_in")
            sp.wait_ge(S["pad_set"], 1)
            sp.dma_start(a["slots"][DUMMY:DUMMY + P, :], pad[:]).then_inc(S["pads_in"], 16)
            sp.dma_start(a["acc"][T:T + P, :], pad[:, 0:D]).then_inc(S["acc_in"], 16)
            sp.wait_ge(S["tabled"], 1)
            for e in range(E):
                c = sp.value_load(count_i[0:1, e:e + 1], min_val=0, max_val=T)
                sp.dma_start(a["slots"][ds(c + e * REGION, P), :], pad[:]).then_inc(S["pads_in"], 16)
            sp.wait_ge(S["sent_ready"], 1)
            load(be1r, a["be1"].broadcast_to([P, E * HID]), "late_in")
            load(be2r, a["be2"].broadcast_to([P, E * D]), "late_in")
            sp.wait_ge(S["pads_in"], 16 * (E + 1))
            for i in range(SENDS):
                sp.wait_ge(S[f"scatter{i}"], 16 * 2 * len(range(i, GROUPS, SENDS)))

            def tile_load(j, u):
                r = sp.value_load(table[0:1, ds(j, 1)], min_val=0, max_val=DUMMY)
                wait(sp, S["xet_done"], j - 3)
                wait(sp, S["meta_done"], j - 3)
                sp.dma_start(xe[u], a["slots"][ds(r, P), :]).then_inc(S[f"xe{u}_in"], 16)

            for j in range(4):
                tile_load(j, j)
            with sp.Fori(1, TILES // 4) as q:
                for u in range(4):
                    tile_load(q * 4 + u, u)
            for j in range(TILES // 4 * 4, TILES):
                tile_load(j, j % 4)
            sp.wait_ge(S["added"], 16 * TILES)

        @block.tensor
        def _(pe):
            mm = nc.tensor.matmul

            def embed(i, m, ks=range(KP)):
                pe.wait_ge(S["patch_in"], 16 * (i + 1))
                for k in ks:
                    last = mm(bank[4][:, m * 2 * NG:(m + 1) * 2 * NG], w1[:, k, m * P:(m + 1) * P], patch[:, k, :],
                              start=k == 0, stop=k == KP - 1)
                if k == KP - 1:
                    last.then_inc(S["emb_done"], 1)

            def embed_ahead(G, ks):
                if G.exists and ahead(G):
                    number, i, m = ahead(G)
                    pe.wait_ge(S["pre_done"], number)
                    embed(i, m, ks)

            def token(G):
                n = G.n
                if G.is_number(0):
                    pe.wait_ge(S["w2_in"], 16)
                    pe.wait_ge(S["prep_dve"], 1)
                pe.wait_ge(S["silu_done"], G.turn + 1)
                wait(pe, S["rt_ready"], G.g - 1)
                for c in range(CD):
                    last = mm(bank[5][0:n, 0:D], silu[:, c, G.r * NG:G.r * NG + n], w2[:, c, :], start=c == 0,
                              stop=c == CD - 1)
                last.then_inc(S["tok_done"], 1)

            def norm1_t(G):
                n = G.n
                if G.is_number(0):
                    pe.wait_ge(S["const_in"], 16)
                pe.wait_ge(S["ln1_done"], G.g + 1)
                wait(pe, S["probt_ready"], (G.g - 1) * 4 + 2)
                for c in range(CD):
                    last = nc.tensor.transpose(bank[1][:, c * NG:c * NG + n], xn[0:n, c * P:(c + 1) * P],
                                               ident[0:n, 0:n])
                last.then_inc(S["t1_done"], 1)

            def project_qk(b, first, n):
                for c in range(CD):
                    m = first + c
                    for k in range(CD):
                        last = mm(bank[b][:, c * NG:c * NG + n], wqk[:, k, m * P:(m + 1) * P], xn_t[:, k, 0:n],
                                  start=k == 0, stop=k == CD - 1)
                last.then_inc(S["qk_done"], 1)

            def keys(G):
                if G.is_number(0):
                    pe.wait_ge(S["wqk_in"], 16)
                pe.wait_ge(S["xnt_ready"], G.g + 1)
                project_qk(1, CD, G.n)

            def queries(G):
                wait(pe, S["probt_ready"], G.g * 4)
                project_qk(0, 0, G.n)

            def own_values(G):
                n = G.n
                if G.is_number(0):
                    pe.wait_ge(S["wv_in"], 16)
                wait(pe, S["xn2t_ready"], G.g - 1)
                wait(pe, S["v_ready"], G.g)
                for k in range(CD):
                    last = mm(bank[6][0:n, D:2 * D], xn_t[:, k, 0:n], wv[:, k, :], start=k == 0, stop=k == CD - 1)
                last.then_inc(S["v_done"], 1)

            def scores(G):
                n = G.n
                pe.wait_ge(S["q_ready"], G.g + 1)
                for j in range(H // QUART):
                    pe.wait_ge(S["km_ready"], G.g * CD + j * QUART // HC + 1)
                    wait(pe, S["probt_ready"], (G.g - 1) * 4 + j + 1)
                    o = view(j, QUART, n)[0:n]
                    c = j * QUART // HC
                    mm(o, q_t[G.par][:, c, 0:n], km[G.par][:, j * QUART:(j + 1) * QUART, 0:n], start=True,
                       stop=True).then_inc(S["score_done"], 1)

            def probs_t(G, j):
                n = G.n
                pe.wait_ge(S["exp_done"], G.g * 4 + j + 1)
                for i in range(QUART):
                    last = nc.tensor.transpose(bank[j][0:n, i * NG:i * NG + n], prob[0:n, j * QUART + i, 0:n],
                                               ident[0:n, 0:n])
                last.then_inc(S["pt_done"], 1)

            def values(G, j):
                n = G.n
                pe.wait_ge(S["v_ready"], G.g + 1)
                wait(pe, S["attt_ready"], G.g)
                c = j * QUART // HC
                pe.wait_ge(S["probt_ready"], G.g * 4 + j + 1)
                for b in range(QUART):
                    h, second = head_at(j * QUART + b), j % 2
                    at = DH + h * VSTEP - DH * second
                    last = mm(bank[7][b * BLOCK:(b + 1) * BLOCK, c * NG:c * NG + n],
                              v_wide[G.par][0:n, at:at + BLOCK], prob_t[0:n, j * QUART + b, 0:n],
                              start=not second, stop=bool(second))
                if j == H // QUART - 1:
                    last.then_inc(S["pv_done"], 1)

            def sums_t(G):
                n = G.n
                pe.wait_ge(S["rsum_done"], G.g * 3 + 3)
                pe.wait_ge(S["ln1_done"], at_most(G.g + 2, GROUPS))
                for c in range(CD):
                    last = nc.tensor.transpose(bank[5][:, c * NG:c * NG + n],
                                               rsum_w[0:n, c * HC:(c + 1) * HC, :].rearrange("p h d -> p (h d)"),
                                               ident[0:n, 0:n])
                last.then_inc(S["rt_done"], 1)

            def project(G):
                n = G.n
                if G.is_number(0):
                    pe.wait_ge(S["wo_in"], 16)
                pe.wait_ge(S["attt_ready"], G.g + 1)
                pe.wait_ge(S["v_ready"], G.g + 1)
                wait(pe, S["xn2t_ready"], G.g)
                for c in range(CD):
                    last = mm(bank[6][0:n, 0:D], att_t[:, c, 0:n], wo[:, c, :], start=c == 0, stop=c == CD - 1)
                last.then_inc(S["o_done"], 1)

            def norm2_t(G):
                n = G.n
                pe.wait_ge(S["ln2_done"], G.g + 1)
                pe.wait_ge(S["v_ready"], at_most(G.g + 2, GROUPS))
                for c in range(CD):
                    last = nc.tensor.transpose(bank[6][:, c * NG:c * NG + n], xn2[0:n, c * P:(c + 1) * P],
                                               ident[0:n, 0:n])
                last.then_inc(S["t3_done"], 1)

            def hidden(G, w):
                n = G.n2
                for m in range(CH):
                    at = m % 2 * 2 * NG
                    for k in range(CD):
                        last = mm(bank[2 * G.par + m // 2][:, at:at + n], w[:, k, m * P:(m + 1) * P],
                                  xn2t_all[:, k, ds(G.g * 2 * NG, n)], start=k == 0, stop=k == CD - 1)
                return last

            def route_hidden(G):
                wait(pe, S["gelu_done"], G.g - 1)
                hidden(G, gw1).then_inc(S["gh_done"], 1)

            def start_b(i):
                pe.wait_ge(S["gw1_in"], 16)
                pe.wait_ge(S["xn2t_ready"], 2 * (i + 1))
                pe.wait_ge(S["probt_ready"], 4 * GROUPS)
                route_hidden(Group(2, 0, i, PAIRS))

            def step_a(at):
                new, mid, old = at(0), at(1), at(2)
                if new.exists:
                    token(new)
                if new.is_number(0):
                    pe.wait_ge(S["pre_done"], CD)
                    embed(1, 0)
                    norm1_t(new)
                    keys(new)
                    queries(new)
                    embed_ahead(new, range(KP))
                    return
                if mid.exists:
                    scores(mid)
                if old.exists:
                    project(old)
                if old.is_number(GROUPS - 1):
                    start_b(0)
                if mid.exists:
                    own_values(mid)
                    probs_t(mid, 0)
                embed_ahead(new, range(0, 1))
                if mid.exists:
                    probs_t(mid, 1)
                    values(mid, 0)
                embed_ahead(new, range(1, 3))
                if mid.exists:
                    probs_t(mid, 2)
                    values(mid, 1)
                    probs_t(mid, 3)
                    values(mid, 2)
                if new.exists:
                    norm1_t(new)
                if mid.exists:
                    values(mid, 3)
                embed_ahead(new, range(3, 4))
                if new.exists:
                    keys(new)
                if mid.exists:
                    sums_t(mid)
                if new.exists:
                    queries(new)
                embed_ahead(new, range(4, KP))
                if old.exists:
                    norm2_t(old)
                if old.is_number(GROUPS - 1):
                    start_b(1)

            pe.wait_ge(S["w1_in"], 16)
            for m in range(CD):
                embed(0, m)
            pipeline(pe, step_a, 2, reach=2)

            def route_logits(G):
                n = G.n2
                pe.wait_ge(S["gelu_done"], G.g + 1)
                wait(pe, S["logit_out"], G.g - 1)
                for c in range(CH):
                    last = mm(bank[4 + G.par][0:E, 0:n], gw2[:, c, :], gh[G.par][:, c, 0:n], start=c == 0,
                              stop=c == CH - 1)
                last.then_inc(S["logit_done"], 1)

            def logits_t(G):
                if G.is_number(0):
                    pe.wait_ge(S["xn2t_ready"], GROUPS)
                wait(pe, S["choose"], ((G.g - 2) * 2 + 1) * CHOOSE + 1)
                wait_alone(pe, S["logit_out"], G.g + 1)
                for i in range(2):
                    n = G.group(i).n
                    last = nc.tensor.transpose(bank[6 + G.par][0:n, i * E:(i + 1) * E],
                                               logit_t[G.par][:, i * NG:i * NG + n], ident[0:E, 0:E])
                last.then_inc(S["logitt_done"], 1)

            def shared_hidden(G):
                wait(pe, S["shgelu_done"], G.g - 1)
                hidden(G, ws1).then_inc(S["sh_done"], 1)

            def step_b(at):
                new, mid, old = at(0), at(1), at(2)
                if new.exists and not (new.is_number(0) or new.is_number(1)):
                    route_hidden(new)
                if mid.exists:
                    route_logits(mid)
                if old.is_number(PAIRS - 1):
                    pe.wait_ge(S["ws1_in"], 16)
                    pe.wait_ge(S["gelu_done"], PAIRS)
                    shared_hidden(Group(2, 0, 0, PAIRS))
                if old.exists:
                    logits_t(old)

            pe.wait_ge(S["gw2_in"], 16)
            pe.wait_ge(S["rt_ready"], GROUPS)
            pipeline(pe, step_b, 2, PAIRS)

            def rank():
                pe.wait_ge(S["route"], COUNTED)
                ranks = bank[6][0:NG, 0:GROUPS * E]
                mm(ranks, tri[0:NG, 0:NG], chosen[0:NG].rearrange("p g e -> p (g e)"), start=True, stop=False)
                mm(ranks, ones[0:NG, 0:NG], before[1][0:NG].rearrange("p g e -> p (g e)"), start=False,
                   stop=True).then_inc(S["rank_done"], 1)
                mm(bank[7][0:1, 0:E], ones[0:NG, 0:1], count_all[0:NG, :], start=True, stop=True).then_inc(
                    S["totals_done"], 1)

            def shared_out(G):
                if G.is_number(0):
                    pe.wait_ge(S["choose"], CHOOSE * GROUPS)
                pe.wait_ge(S["shgelu_done"], G.g + 1)
                wait(pe, S["acc_ready"], G.g - 1)
                for i in range(2):
                    n = G.group(i).n
                    for c in range(CH):
                        last = mm(bank[4 + G.par][0:n, i * D:(i + 1) * D], gh[G.par][:, c, i * NG:i * NG + n],
                                  ws2[:, c, :], start=c == 0, stop=c == CH - 1)
                last.then_inc(S["so_done"], 1)

            def step_c(at):
                if at(0).exists and not at(0).is_number(0):
                    shared_hidden(at(0))
                if at(0).is_number(1):
                    rank()
                if at(1).exists:
                    shared_out(at(1))

            pe.wait_ge(S["ws2_in"], 16)
            pipeline(pe, step_c, 1, PAIRS)

            pe.wait_ge(S["tabled"], 1)
            pe.wait_ge(S["we1_in"], 16)
            pe.wait_ge(S["late_in"], 48)
            pe.wait_ge(S["shgelu_done"], PAIRS)

            def expert_of(G):
                return pe.value_load(table[0:1, ds(G.g + TILES, 1)], min_val=0, max_val=E - 1)

            def rows_t(G):
                u4 = G.r
                wait(pe, S["xet_ready"], G.g - 1)
                pe.wait_ge(S[f"xe{u4}_in"], 16 * G.use(4))
                for c in range(CD):
                    last = nc.tensor.transpose(bank[G.par][:, c * P:(c + 1) * P], xe[u4][:, c * P:(c + 1) * P],
                                               ident[:, :])
                last.then_inc(S["xet_done"], 1)

            def up(G):
                e = expert_of(G)
                pe.wait_ge(S["xet_ready"], G.g + 1)
                wait(pe, S["epre_done"], G.g - 1)
                for k in range(CD):
                    last = mm(bank[2 + G.par][:, :], xe_t[G.par][:, k, :], we1[:, ds(e * (CD * HID) + k * HID, HID)],
                              start=k == 0, stop=k == CD - 1)
                last.then_inc(S["eh_done"], 1)

            def hidden_t(G):
                if G.is_number(0):
                    pe.wait_ge(S["acc_ready"], PAIRS)
                pe.wait_ge(S["egelu_done"], G.g + 1)
                wait(pe, S["eht_ready"], G.g - 1)
                for c in range(CH):
                    last = nc.tensor.transpose(bank[4 + G.par][:, c * P:(c + 1) * P], ehid[G.par][:, c * P:(c + 1) * P],
                                               ident[:, :])
                last.then_inc(S["eht_done"], 1)

            def down(G):
                e = expert_of(G)
                pe.wait_ge(S["eht_ready"], G.g + 1)
                wait(pe, S["ey_steps"], (G.g - 2) * 2 + 1)
                for c in range(CH):
                    last = mm(bank[6 + G.par][:, 0:D], ehid_t[G.par][:, c, :], we2[:, ds(e * (CH * D) + c * D, D)],
                              start=c == 0, stop=c == CH - 1)
                last.then_inc(S["ey_done"], 1)

            def step_d(at):
                if at(1).exists:
                    up(at(1))
                if at(0).exists:
                    rows_t(at(0))
                if at(3).exists:
                    down(at(3))
                if at(2).exists:
                    hidden_t(at(2))

            pipeline(pe, step_d, 3, TILES, 4)

        @block.scalar
        def _(act):
            def act_tanh(i):
                wait(act, S["silu_done"], i)
                act.wait_ge(S["pre_done"], (i + 1) * CD)
                nc.scalar.activation(tanh_h[:], pre[:], ACT.Tanh, scale=0.5).then_inc(S["tanh_done"], 1)

            def act_rt(G):
                act.wait_ge(S["rt_done"], G.g + 1)
                nc.scalar.copy(rsum_t[:, :, 0:G.n], view(5, CD, G.n)).then_inc(S["rt_ready"], 1)

            def act_exp(G, j):
                n = G.n
                act.wait_ge(S["diff_done"], G.g * 4 + j + 1)
                pj = prob[0:n, j * QUART:(j + 1) * QUART, 0:n]
                nc.scalar.activation(pj, pj, ACT.Exp, scale=DH ** -0.5).then_inc(S["exp_done"], 1)

            def act_probt(G, j):
                n = G.n
                act.wait_ge(S["pt_done"], G.g * 4 + j + 1)
                wait(act, S["pv_done"], G.g)
                nc.scalar.copy(prob_t[0:n, j * QUART:(j + 1) * QUART, 0:n], view(j, QUART, n)[0:n]).then_inc(
                    S["probt_ready"], 1)

            def act_xnt(G):
                act.wait_ge(S["t1_done"], G.g + 1)
                wait(act, S["v_done"], G.g)
                nc.scalar.copy(xn_t[:, :, 0:G.n], view(1, CD, G.n)).then_inc(S["xnt_ready"], 1)

            def act_xn2t(G):
                act.wait_ge(S["t3_done"], G.g + 1)
                nc.scalar.copy(xn2t_all[:, :, ds(G.g * NG, G.n)], view(6, CD, G.n)).then_inc(S["xn2t_ready"], 1)

            def act_qk(G, i, dst, b):
                n = G.n
                act.wait_ge(S["qk_done"], G.g * 2 + i + 1)
                for c in range(CD):
                    m = (1 - i) * CD + c
                    last = nc.scalar.activation(dst[:, c, 0:n], bank[b][:, c * NG:c * NG + n], ACT.Identity,
                                                bias=qkbc[:, m:m + 1])
                last.then_inc(S["q_ready" if i else "k_ready"], 1)

            def step_a(at):
                new, mid, old = at(0), at(1), at(2)
                if silu_due(new):
                    act_tanh(new.turn + 1)
                if mid.exists:
                    act_exp(mid, 0)
                    act_exp(mid, 1)
                    act_probt(mid, 0)
                    act_exp(mid, 2)
                    act_probt(mid, 1)
                    act_exp(mid, 3)
                    act_probt(mid, 2)
                    act_probt(mid, 3)
                if new.exists:
                    act_xnt(new)
                    wait(act, S["km_ready"], new.g * CD)
                    act_qk(new, 0, k_t, 1)
                if mid.exists:
                    act_rt(mid)
                if new.exists:
                    act_qk(new, 1, q_t[new.par], 0)
                if old.is_number(GROUPS - 1):
                    nc.scalar.activation(warm[:], cols[:, 0:1], ACT.Gelu)
                if old.exists:
                    act_xn2t(old)

            act.wait_ge(S["cols_in"], 16)
            nc.scalar.activation(warm[:], cols[:, 0:1], ACT.Tanh)
            act_tanh(0)
            pipeline(act, step_a, 2)

            def act_gelu(G):
                act.wait_ge(S["gh_done"], G.g + 1)
                wait(act, S["logit_done"], G.g - 1)
                gelu(G, ACT.Gelu, gb1c).then_inc(S["gelu_done"], 1)

            def gelu(G, function, bias):
                n = G.n2
                for m in range(CH):
                    at = m % 2 * 2 * NG
                    last = nc.scalar.activation(gh[G.par][:, m, 0:n], bank[2 * G.par + m // 2][:, at:at + n],
                                                function, bias=bias[:, m:m + 1])
                return last

            def step_b(at):
                if at(0).exists:
                    act_gelu(at(0))

            pipeline(act, step_b, 2, PAIRS)
            act.wait_ge(S["choose"], CHOOSE * GROUPS)
            nc.scalar.activation(num[0:NG], num[0:NG], ACT.Exp).then_inc(S["gate_exp_done"], 1)

            def act_shared(G):
                act.wait_ge(S["sh_done"], G.g + 1)
                act.wait_ge(S["logit_done"], PAIRS)
                wait(act, S["so_done"], G.g - 1)
                gelu(G, ACT.Gelu_apprx_tanh, bs1c).then_inc(S["shgelu_done"], 1)

            def acc_store(G):
                act.wait_ge(S["acc_ready"], G.g + 1)
                if G.n2 == 2 * NG:
                    src = resid[0:NG, ds(G.g * 2 * D, 2 * D)].rearrange("p (i d) -> p i d", i=2)
                    act.dma_start(a["acc"][ds(G.g * 2 * NG, 2 * NG), :].rearrange("(i p) d -> p i d", i=2),
                                  src).then_inc(S["acc_in"], 16)
                    return
                for i in range(2):
                    last = G.group(i)
                    act.dma_start(a["acc"][ds(last.g * NG, last.n), :],
                                  resid[0:last.n, ds(last.g * D, D)]).then_inc(S["acc_in"], 16)

            def step_c(at):
                if at(0).exists:
                    act_shared(at(0))
                if at(2).exists and not at(2).is_number(PAIRS - 1):
                    acc_store(at(2))

            pipeline(act, step_c, 2, PAIRS)

            def act_rows(G):
                act.wait_ge(S["xet_done"], G.g + 1)
                nc.scalar.copy(xe_t[G.par][:, :, :], bank[G.par][:, 0:D].rearrange("p (c n) -> p c n", c=CD)).then_inc(
                    S["xet_ready"], 1)

            def act_egelu(G):
                act.wait_ge(S["epre_done"], G.g + 1)
                wait(act, S["eht_done"], G.g - 1)
                nc.scalar.activation(ehid[G.par][:, :], epre[:, :], ACT.Gelu_apprx_tanh).then_inc(S["egelu_done"], 1)

            def step_d(at):
                if at(0).exists:
                    act_rows(at(0))
                if at(0).is_number(0):
                    acc_store(Group(2, 0, PAIRS - 1, PAIRS))
                if at(1).exists:
                    act_egelu(at(1))

            pipeline(act, step_d, 3, TILES, 4)

        @block.vector
        def _(dve):
            V = nc.vector

            dve.wait_ge(S["const_in"], 16)
            dve.wait_ge(S["w2_in"], 16)
            V.tensor_scalar(w2, w2, 0.5, None, ALU.mult)
            V.memset(ones[:], 1.0).then_inc(S["prep_dve"], 1)

            def dve_pre(i, m, done):
                dve.wait_ge(S["emb_done"], done)
                wait(dve, S["silu_done"], i)
                V.tensor_scalar(pre[:, m, :], bank[4][:, m * 2 * NG:(m + 1) * 2 * NG], b1c[:, m:m + 1], None,
                                ALU.add).then_inc(S["pre_done"], 1)

            def pre_ahead(G):
                if ahead(G):
                    number, i, m = ahead(G)
                    dve_pre(i, m, number + 1)

            def dve_silu(i):
                dve.wait_ge(S["tanh_done"], i + 1)
                wait(dve, S["tok_done"], i * 2)
                V.scalar_tensor_tensor(out=silu[:], in0=tanh_h[:], scalar=1.0, in1=pre[:],
                                       op0=ALU.add, op1=ALU.mult).then_inc(S["silu_done"], 1)

            def masked(G, j):
                n = G.n
                dve.wait_ge(S["score_done"], G.g * 4 + j + 1)
                wait(dve, S["pt_done"], (G.g - 1) * 4 + j + 1)
                wait(dve, S["rsum_done"], (G.g - 1) * 3 + 1)
                mask = spread(const[0:n, C_MASK:C_MASK + n], [n, QUART, n])
                V.tensor_tensor(prob[0:n, j * QUART:(j + 1) * QUART, 0:n], view(j, QUART, n)[0:n], mask,
                                ALU.add).then_inc(S["mask_done"], 1)

            def largest(G, j):
                n = G.n
                dve.wait_ge(S["mask_done"], G.g * 4 + j + 1)
                wait(dve, S["diff_done"], (G.g - 1) * 4 + j + 1)
                V.reduce_max(smax[0:n, j * QUART:(j + 1) * QUART], prob[0:n, j * QUART:(j + 1) * QUART, 0:n],
                             AX.X).then_inc(S["smax_done"], 1)

            def dve_token(G):
                n = G.n
                dve.wait_ge(S["tok_done"], G.g + 1)
                wait(dve, S["base_done"], G.g)
                V.tensor_tensor(tok[0:n, :], bank[5][0:n, 0:D], b2r[0:n, :], ALU.add).then_inc(S["ln1_stat"], 1)

            def token_sums(G):
                wait_alone(dve, S["ln1_stat"], G.g * 3 + 1)
                V.bn_stats(stat[0:G.n, 0, :], tok[0:G.n, :]).then_inc(S["ln1_stat"], 1)

            def token_mean(G):
                wait_alone(dve, S["ln1_stat"], G.g * 3 + 2)
                V.bn_aggr(mv[0:G.n, 0, :], stat[0:G.n, 0:1, :]).then_inc(S["ln1_stat"], 1)

            def dve_norm1(G):
                n = G.n
                dve.wait_ge(S["ln1_rstd"], G.g * 2 + 2)
                wait(dve, S["t1_done"], G.g)
                V.tensor_scalar(xn[0:n, :], tok[0:n, :], mv[0:n, 0, 0:1], rstd[0:n, 0, :], ALU.subtract,
                                ALU.mult).then_inc(S["ln1_done"], 1)

            def dve_residual(G):
                n = G.n
                r = resid[0:n, ds(G.g * D, D)]
                dve.wait_ge(S["o_done"], G.g + 1)
                dve.wait_ge(S["base_done"], G.g + 1)
                V.tensor_tensor(r, bank[6][0:n, 0:D], r, ALU.add).then_inc(S["x1_done"], 1)
                wait_alone(dve, S["x1_done"], G.g + 1)
                V.bn_stats(stat[0:n, 1, :], r).then_inc(S["ln2_stat"], 1)
                wait_alone(dve, S["ln2_stat"], G.g * 2 + 1)
                V.bn_aggr(mv[0:n, 1, :], stat[0:n, 1:2, :]).then_inc(S["ln2_stat"], 1)

            def dve_norm2(G):
                n = G.n
                dve.wait_ge(S["ln2_rstd"], G.g * 2 + 2)
                wait(dve, S["t3_done"], G.g)
                wait(dve, S["routed_ready"], G.g)
                V.tensor_scalar(xn2[0:n, :], resid[0:n, ds(G.g * D, D)], mv[0:n, 1, 0:1], rstd[0:n, 1, :],
                                ALU.subtract, ALU.mult).then_inc(S["ln2_done"], 1)

            def dve_sums(G):
                n = G.n
                r = S["rsum_done"]
                dve.wait_ge(S["exp_done"], G.g * 4 + 4)
                for c in range(CD):
                    last = V.reduce_sum(rsum[0:n, c * HC:(c + 1) * HC].rearrange("p (b s) -> p s b", s=2),
                                        prob[0:n, c * HC:(c + 1) * HC, 0:n].rearrange("p (s b) k -> p s b k", s=2),
                                        AX.X)
                last.then_inc(r, 1)
                dve.wait_ge(r, G.g * 3 + 1)
                V.reciprocal(rsum[0:n, :], rsum[0:n, :]).then_inc(r, 1)
                dve.wait_ge(r, G.g * 3 + 2)
                wait(dve, S["rt_done"], G.g)
                V.tensor_copy(rsum_w[0:n, :, :], spread_in(rsum[0:n, :], [n, H, DH])).then_inc(r, 1)

            def dve_attention(G):
                n = G.n
                dve.wait_ge(S["pv_done"], G.g + 1)
                dve.wait_ge(S["rt_ready"], G.g + 1)
                wait(dve, S["o_done"], G.g)
                V.tensor_tensor(att_t[:, :, 0:n], view(7, CD, n), rsum_t[:, :, 0:n], ALU.mult).then_inc(
                    S["attt_ready"], 1)

            def dve_values(G):
                n = G.n
                dve.wait_ge(S["v_done"], G.g + 1)
                dst = v_wide[G.par][0:n, DH:].rearrange("p (h d) -> p h d", d=VSTEP)[:, :, 0:DH]
                V.tensor_tensor(dst, bank[6][0:n, D:2 * D].rearrange("p (h d) -> p h d", d=DH),
                                vbr[0:n, :].rearrange("p (h d) -> p h d", d=DH), ALU.add).then_inc(S["v_ready"], 1)

            def step_a(at):
                new, mid, old = at(0), at(1), at(2)
                if new.exists:
                    dve_token(new)
                if mid.exists:
                    masked(mid, 0)
                if new.exists:
                    token_sums(new)
                if mid.exists:
                    largest(mid, 0)
                if new.exists:
                    token_mean(new)
                if mid.exists:
                    masked(mid, 1)
                    largest(mid, 1)
                    masked(mid, 2)
                    largest(mid, 2)
                    dve_values(mid)
                    masked(mid, 3)
                    largest(mid, 3)
                if new.exists:
                    dve_norm1(new)
                if new.is_number(0):
                    dve_pre(1, 0, 3)
                if old.exists:
                    dve_residual(old)
                if mid.exists:
                    dve_sums(mid)
                if old.exists:
                    dve_norm2(old)
                if silu_due(new):
                    dve_silu(new.turn + 1)
                if mid.exists:
                    dve_attention(mid)
                if new.exists:
                    pre_ahead(new)

            dve.wait_ge(S["cols_in"], 16)
            dve.wait_ge(S["rows_in"], 16)
            dve.wait_ge(S["v_zeroed"], 1)
            for m in range(CD):
                dve_pre(0, m, CD)
            dve_silu(0)
            pipeline(dve, step_a, 2, reach=2)

            def dve_logits(G):
                wait(dve, S["logitt_done"], G.g - 1)
                dve.wait_ge(S["logit_done"], G.g + 1)
                V.tensor_scalar(logit_t[G.par][:, 0:G.n2], bank[4 + G.par][0:E, 0:G.n2], gb2c, None,
                                ALU.add).then_inc(S["logit_out"], 1)

            def choose(pair, i):
                G = pair.group(i)
                n = G.n
                r = S["choose"]
                dve.wait_ge(S["logitt_done"], pair.g + 1)
                V.tensor_copy(logit[0:n, :], bank[6 + pair.par][0:n, i * E:(i + 1) * E]).then_inc(r, 1)
                wait_alone(dve, r, G.g * CHOOSE + 1)
                V.max(order[0:n, :], logit[0:n, :]).then_inc(r, 1)
                wait_alone(dve, r, G.g * CHOOSE + 2)
                V.max_index(whose[0:n, :], order[0:n, :], logit[0:n, :]).then_inc(r, 1)
                V.tensor_scalar(of_group(num, E, G), logit[0:n, :], order[0:n, 0:1], None, ALU.subtract).then_inc(r, 1)
                dve.wait_ge(r, G.g * CHOOSE + 4)
                V.tensor_copy(of_group(topf, 2, G), whose[0:n, 0:2]).then_inc(r, 1)

            def of_group(x, width, G):
                return x[0:G.n].rearrange("p g e -> p (g e)")[:, ds(G.g * width, width)]

            def step_b(at):
                if at(1).exists:
                    dve_logits(at(1))
                if at(2).exists:
                    choose(at(2), 0)
                    choose(at(2), 1)

            dve.wait_ge(S["pv_done"], GROUPS)
            V.memset(num[:, GROUPS - 1, :], 0.0)
            V.memset(topf[:, GROUPS - 1, :], 0.0).then_inc(S["prep_dve"], 1)
            dve.wait_ge(S["prep_dve"], 2)
            pipeline(dve, step_b, 2, PAIRS)

            def dve_shared(pair):
                dve.wait_ge(S["so_done"], pair.g + 1)
                out = bank[4 + pair.par]
                if pair.n2 == 2 * NG:
                    r = resid[0:NG, ds(pair.g * 2 * D, 2 * D)]
                    V.tensor_tensor(r, out[0:NG, :], r, ALU.add).then_inc(S["acc_ready"], 1)
                    return
                for i in range(2):
                    G = pair.group(i)
                    r = resid[0:G.n, ds(G.g * D, D)]
                    last = V.tensor_tensor(r, out[0:G.n, i * D:(i + 1) * D], r, ALU.add)
                last.then_inc(S["acc_ready"], 1)

            rt = S["route"]
            nth = [0]

            def after(instruction):
                nth[0] += 1
                instruction.then_inc(rt, 1)
                dve.wait_ge(rt, nth[0])

            dve.wait_ge(S["choose"], CHOOSE * GROUPS)
            a2 = lambda x: x[0:NG]
            four = [NG, GROUPS, 2, E]
            iota4 = const[0:NG, C_IOTA:C_IOTA + E].unsqueeze(1).unsqueeze(1).broadcast_to(four)
            after(V.tensor_tensor(a2(hot), iota4, a2(topf).unsqueeze(3).broadcast_to(four), ALU.is_equal))
            after(V.tensor_tensor(a2(chosen), a2(hot)[:, :, 0, :], a2(hot)[:, :, 1, :], ALU.add))
            after(V.tensor_scalar(a2(chosen)[:, GROUPS - 1, :], a2(chosen)[:, GROUPS - 1, :],
                                  const[0:NG, C_VALID:C_VALID + 1], None, ALU.mult))
            V.memset(before[0][:, 0:1, :], 0.0)
            after(V.tensor_copy(a2(before[0])[:, 1:, :], a2(chosen)[:, 0:GROUPS - 1, :]))
            for i in range(DOUBLINGS):
                old, new, by = a2(before[i % 2]), a2(before[(i + 1) % 2]), 1 << i
                V.tensor_copy(new[:, 0:by, :], old[:, 0:by, :])
                after(V.tensor_tensor(new[:, by:, :], old[:, by:, :], old[:, 0:GROUPS - by, :], ALU.add))
            after(V.tensor_tensor(count_all[0:NG, :], a2(before[1])[:, GROUPS - 1, :], a2(chosen)[:, GROUPS - 1, :],
                                  ALU.add))
            assert nth[0] == COUNTED, nth[0]
            dve.wait_ge(S["gate_exp_done"], 1)
            after(V.reduce_sum(a2(gsum).rearrange("p g e -> p (g e)"), a2(num), AX.X))
            after(V.reciprocal(a2(gsum), a2(gsum)))
            rows_out = routed[0:NG, :].rearrange("p (g r) -> p g r", g=GROUPS)
            V.tensor_copy(rows_out[:, :, D:D + 1], const[0:NG, C_TOK:C_TOK + GROUPS].unsqueeze(2))
            after(V.tensor_tensor(rows_out[:, :, D + 1:], a2(num), a2(gsum).broadcast_to([NG, GROUPS, E]), ALU.mult))

            dve.wait_ge(S["routed_ready"], GROUPS)
            dve.wait_ge(S["pool_steps"], GROUPS)

            dve.wait_ge(S["rank_done"], 1)
            after(V.tensor_tensor(a2(place_of), bank[6][0:NG, 0:GROUPS * E].rearrange("p (g e) -> p g e", e=E),
                                  spread(const[0:NG, C_BASE:C_BASE + E], [NG, GROUPS, E]), ALU.add))
            after(V.tensor_tensor(a2(hot_place), a2(hot), a2(place_of).unsqueeze(2).broadcast_to(four), ALU.mult))
            after(V.reduce_sum(slot_f[0:NG, :], a2(hot_place).rearrange("p g k e -> p (g k) e"), AX.X))

            st = S["table_steps"]
            done = [0]

            def then(instruction):
                done[0] += 1
                instruction.then_inc(st, 1)
                dve.wait_ge(st, done[0])

            def by_expert(x):
                return spread(x, [1, TILES, E])

            def table_first():
                dve.wait_ge(S["totals_done"], 1)
                then(V.tensor_copy(counts, bank[7][0:1, 0:E]))
                then(V.tensor_copy(count_i[:, 0:E], counts))
                then(V.tensor_scalar(wt, counts, float(P - 1), None, ALU.add))
                then(V.tensor_copy(count_i[:, E:2 * E], wt))
                then(V.tensor_scalar(count_i[:, E:2 * E], count_i[:, E:2 * E], 7, None, ALU.logical_shift_right))
                then(V.tensor_copy(ntile, count_i[:, E:2 * E]))
                ltv = lt_tmp[:, :].rearrange("p (a b) -> p a b", b=E)
                then(V.tensor_tensor(ltv, const[0:1, C_LT:C_LT + E * E].rearrange("p (a b) -> p a b", b=E),
                                     spread(ntile, [1, E, E]), ALU.mult))
                then(V.reduce_sum(start_t, ltv, AX.X))
                then(V.tensor_tensor(end_t, start_t, ntile, ALU.add))
                then(V.scalar_tensor_tensor(out=wt, in0=start_t, scalar=-float(P), in1=const[0:1, C_BASE:C_BASE + E],
                                            op0=ALU.mult, op1=ALU.add))

            def table_rest():
                jv = const[0:1, C_J:C_J + TILES * E].rearrange("p (j e) -> p j e", e=E)
                then(V.tensor_tensor(tb[0], jv, by_expert(start_t), ALU.is_ge))
                then(V.tensor_tensor(tb[1], jv, by_expert(end_t), ALU.is_lt))
                then(V.tensor_tensor(tb[0], tb[0], tb[1], ALU.mult))
                then(V.scalar_tensor_tensor(out=tb[2], in0=jv, scalar=float(P), in1=by_expert(wt), op0=ALU.mult,
                                            op1=ALU.add))

            def table_sums():
                then(V.tensor_tensor(tb[3], tb[0], tb[2], ALU.mult))
                then(V.tensor_tensor(tb[4], tb[0], by_expert(const[0:1, C_IOTA:C_IOTA + E]), ALU.mult))
                then(V.reduce_sum(table_f[:, 0:TILES], tb[3], AX.X))
                then(V.reduce_sum(table_f[:, TILES:2 * TILES], tb[4], AX.X))

            def table_idle():
                then(V.reduce_sum(table_f[:, 2 * TILES:], tb[0], AX.X))
                then(V.tensor_scalar(table_f[:, 2 * TILES:], table_f[:, 2 * TILES:], -float(DUMMY), float(DUMMY),
                                     ALU.mult, ALU.add))
                then(V.tensor_tensor(table_f[:, 0:TILES], table_f[:, 0:TILES], table_f[:, 2 * TILES:], ALU.add))
                V.tensor_copy(table[:, :], table_f[:, 0:2 * TILES]).then_inc(S["tabled"], 1)

            def build(pair, i):
                G, slot = pair.group(i), 2 * pair.par + i
                n = G.n
                wait(dve, S[f"scatter{slot}"], (pair.use(2) - 1) * 32)
                V.tensor_copy(sent[slot][0:n, :], routed[0:n, ds(G.g * ROW, ROW)])
                V.tensor_copy(slot_now[slot][0:n, :], slot_f[0:n, ds(G.g * 2, 2)]).then_inc(S["sent_ready"], 1)

            def step_c(at):
                if at(3).exists:
                    dve_shared(at(3))
                if at(0).exists:
                    build(at(0), 0)
                    build(at(0), 1)
                for i, table_part in enumerate((table_first, table_rest, table_sums, table_idle)):
                    if at(0).is_number(i + 1):
                        table_part()

            pipeline(dve, step_c, 3, PAIRS)

            def expert_of(G):
                return dve.value_load(table[0:1, ds(G.g + TILES, 1)], min_val=0, max_val=E - 1)

            def dve_epre(G):
                e = expert_of(G)
                dve.wait_ge(S["eh_done"], G.g + 1)
                wait(dve, S["egelu_done"], G.g)
                V.tensor_tensor(epre[:, :], bank[2 + G.par][:, :], be1r[:, ds(e * HID, HID)], ALU.add).then_inc(
                    S["epre_done"], 1)
                dve.wait_ge(S[f"xe{G.r}_in"], 16 * G.use(4))
                wait(dve, S["added"], (G.g - 3) * 16)
                V.tensor_copy(etok[G.r][:, :], xe[G.r][:, D:D + 1])
                V.tensor_copy(egate[G.r][:, :], xe[G.r][:, ds(e + (D + 1), 1)]).then_inc(S["meta_done"], 1)

            def dve_eht(G):
                dve.wait_ge(S["eht_done"], G.g + 1)
                V.tensor_copy(ehid_t[G.par][:, :, :],
                              bank[4 + G.par][:, :].rearrange("p (c n) -> p c n", c=CH)).then_inc(S["eht_ready"], 1)

            def dve_ey(G):
                e = expert_of(G)
                dve.wait_ge(S["ey_done"], G.g + 1)
                dve.wait_ge(S["meta_done"], G.g + 1)
                V.tensor_tensor(ey[:, :], bank[6 + G.par][:, 0:D], be2r[:, ds(e * D, D)], ALU.add).then_inc(
                    S["ey_steps"], 1)
                wait(dve, S["added"], (G.g - 1) * 16)
                dve.wait_ge(S["ey_steps"], G.g * 2 + 1)
                V.tensor_scalar(eout[G.par][:, :], ey[:, :], egate[G.r][:, :], None, ALU.mult).then_inc(
                    S["ey_steps"], 1)

            def step_d(at):
                if at(3).exists:
                    dve_eht(at(3))
                if at(1).exists:
                    dve_epre(at(1))
                if at(3).exists:
                    dve_ey(at(3))

            dve.wait_ge(S["late_in"], 48)
            pipeline(dve, step_d, 3, TILES, 4)

        @block.gpsimd
        def _(pool):
            G_ = nc.gpsimd
            G_.memset(expo[:], -0.5)
            G_.memset(v_wide[0], 0.0)
            G_.memset(v_wide[1], 0.0).then_inc(S["v_zeroed"], 1)
            G_.memset(pad[:], 0.0).then_inc(S["prep_steps"], 1)
            pool.wait_ge(S["const_in"], 16)
            pool.wait_ge(S["prep_steps"], 1)
            G_.tensor_copy(pad[:, D:D + 1], const[:, C_PADT:C_PADT + 1]).then_inc(S["pad_set"], 1)
            pool.wait_ge(S["rows_in"], 16)

            def pool_rstd(G, i, stat_sem, steps, rstd_sem):
                n = G.n
                wait_alone(pool, S[stat_sem], (G.g + 1) * steps)
                G_.tensor_scalar(rstd[0:n, i, :], mv[0:n, i, 1:2], EPS, None, ALU.add).then_inc(S[rstd_sem], 1)
                pool.wait_ge(S[rstd_sem], G.g * 2 + 1)
                G_.tensor_tensor(rstd[0:n, i, :], rstd[0:n, i, :], expo[0:n, :], ALU.pow).then_inc(S[rstd_sem], 1)

            def pool_below(G, j):
                n = G.n
                pj = prob[0:n, j * QUART:(j + 1) * QUART, 0:n]
                pool.wait_ge(S["smax_done"], G.g * 4 + j + 1)
                G_.tensor_tensor(pj, pj, spread_in(smax[0:n, j * QUART:(j + 1) * QUART], [n, QUART, n]),
                                 ALU.subtract).then_inc(S["diff_done"], 1)

            def pool_base(G):
                n = G.n
                G_.tensor_tensor(resid[0:n, ds(G.g * D, D)], tok[0:n, :], obr[0:n, :], ALU.add).then_inc(
                    S["base_done"], 1)

            def pool_keep(G):
                n = G.n
                r = resid[0:n, ds(G.g * D, D)]
                wait_alone(pool, S["ln2_done"], G.g + 1)
                G_.tensor_copy(routed[0:n, ds(G.g * ROW, D)], xn2[0:n, :]).then_inc(S["routed_ready"], 1)
                G_.tensor_tensor(r, r, bs2r[0:n, :], ALU.add).then_inc(S["pool_steps"], 1)

            def pool_keys(G):
                n = G.n
                pool.wait_ge(S["k_ready"], G.g + 1)
                for c in range(CD):
                    last = G_.tensor_tensor(km[G.par][:, c * HC:(c + 1) * HC, 0:n],
                                            spread(k_t[:, c, 0:n], [P, HC, n]),
                                            spread_in(const[:, C_HEAD:C_HEAD + HC], [P, HC, n]), ALU.mult)
                    last.then_inc(S["km_ready"], 1)

            def step_a(at):
                new, mid, old = at(0), at(1), at(2)
                if mid.exists:
                    pool_below(mid, 0)
                    pool_below(mid, 1)
                if new.exists:
                    pool_rstd(new, 0, "ln1_stat", 3, "ln1_rstd")
                if mid.exists:
                    pool_below(mid, 2)
                    pool_below(mid, 3)
                if old.exists:
                    pool_rstd(old, 1, "ln2_stat", 2, "ln2_rstd")
                if new.exists:
                    pool_base(new)
                    pool_keys(new)
                if old.exists:
                    pool_keep(old)

            pipeline(pool, step_a, 2)

            def send(G):
                n = G.n
                wait_alone(pool, S["sent_ready"], G.g + 1)
                for k in range(2):
                    G_.indirect_dma_start(
                        out=a["slots"],
                        out_offset=bass.IndirectOffsetOnAxis(ap=slot_now[G.r][0:n, k:k + 1], axis=0),
                        in_=sent[G.r][0:n, :], in_offset=None).then_inc(S[f"scatter{G.r}"], 16)

            def step_c(at):
                if at(0).exists:
                    send(at(0))

            pipeline(pool, step_c, 1, GROUPS, SENDS)

            def add_rows(G):
                pool.wait_ge(S["ey_steps"], (G.g + 1) * 2)
                wait_alone(pool, S["added"], G.g * 16)
                G_.indirect_dma_start(
                    out=a["acc"], out_offset=bass.IndirectOffsetOnAxis(ap=etok[G.r][:, 0:1], axis=0),
                    in_=eout[G.par][:, :], in_offset=None, compute_op=ALU.add).then_inc(S["added"], 16)

            def step_d(at):
                if at(3).exists:
                    add_rows(at(3))

            pool.wait_ge(S["acc_in"], 16 * (PAIRS + 1 + 1))
            pipeline(pool, step_d, 3, TILES, 4)
            pool.wait_ge(S["added"], 16 * TILES)


def constants():
    import numpy as np

    c = np.zeros((P, C_N), np.float32)
    q = np.arange(P)
    c[:, C_ID:C_ID + P] = np.eye(P)
    k = np.arange(NG)
    seen = (q[:, None] // SEQ == k[None] // SEQ) & (k[None] <= q[:, None])
    c[:, C_MASK:C_MASK + NG] = np.where(seen, 0.0, -1e30)
    c[:, C_HEAD:C_HEAD + HC] = q[:, None] // DH == np.array([head_at(i) for i in range(HC)])[None]
    c[:, C_TRI:C_TRI + P] = q[:, None] < q[None]
    e = np.arange(E)
    c[:, C_IOTA:C_IOTA + E] = e
    c[:, C_BASE:C_BASE + E] = e * REGION
    c[:, C_LT:C_LT + E * E] = (e[None] < e[:, None]).reshape(-1)
    c[:, C_J:C_J + TILES * E] = np.repeat(np.arange(TILES), E)
    c[:, C_TOK:C_TOK + GROUPS] = np.arange(GROUPS)[None] * NG + q[:, None]
    c[:, C_PADT] = T + q
    c[:, C_VALID] = q < NL
    return c


def kernel(**inputs):
    import numpy as np
    import concourse.bacc as bacc
    from concourse.bass_utils import run_bass_kernel_spmd

    x = {k.replace("L0_", ""): np.asarray(v) for k, v in inputs.items()}
    C, G, PS = 3, 6, 16

    def chunks(w):
        return np.ascontiguousarray(w.reshape(-1, P, w.shape[-1]).transpose(1, 0, 2))

    t = x["x"].reshape(IMAGES, C, G, PS, G, PS).transpose(1, 3, 5, 0, 2, 4).reshape(KP, P, T)
    t = np.pad(t, ((0, 0), (0, 0), (0, GROUPS * NG - T)))
    patch = t.reshape(KP, P, PAIRS, 2 * NG).transpose(2, 1, 0, 3).reshape(PAIRS * P, KP * 2 * NG)
    col = lambda v: v.reshape(-1, P).T
    arrays = {
        "patch": patch,
        "const": constants(),
        "w1": chunks(x["tok_W1"]),
        "w2": chunks(x["tok_W2"]),
        "wqk": chunks(np.concatenate([x["attn_q_w"].T, x["attn_k_w"].T], axis=1)),
        "wv": chunks(x["attn_v_w"].T),
        "wo": chunks(x["attn_o_w"].T),
        "gw1": chunks(x["ffn_gw1"]),
        "gw2": chunks(x["ffn_gw2"]),
        "ws1": chunks(x["ffn_Ws1"]),
        "ws2": chunks(x["ffn_Ws2"]),
        "we1": x["ffn_We1"].reshape(E, CD, P, HID).transpose(2, 0, 1, 3).reshape(P, -1),
        "we2": x["ffn_We2"].reshape(E, CH, P, D).transpose(2, 0, 1, 3).reshape(P, -1),
        "be1": x["ffn_be1"].reshape(1, -1),
        "be2": x["ffn_be2"].reshape(1, -1),
        "cols": np.concatenate([col(x["tok_b1"]), col(x["attn_q_b"]), col(x["attn_k_b"]), col(x["ffn_gb1"]),
                                col(x["ffn_bs1"]), np.pad(x["ffn_gb2"], (0, P - E))[:, None]], axis=1),
        "rows": np.concatenate([x["tok_b2"], x["attn_v_b"], x["attn_o_b"], x["ffn_bs2"]])[None],
    }
    arrays = {f"in_{k}": np.ascontiguousarray(v) for k, v in arrays.items()}
    nc = bacc.Bacc("TRN2", target_bir_lowering=False, num_devices=1)
    a = {k[3:]: nc.dram_tensor(k, v.shape, F32, kind="ExternalInput").ap() for k, v in arrays.items()}
    a["slots"] = nc.dram_tensor("slots", [DUMMY + P, ROW], F32, kind="Internal").ap()
    a["acc"] = nc.dram_tensor("out_acc", [T + P, D], F32, kind="ExternalOutput").ap()
    vit_kernel(nc, a)
    got = run_bass_kernel_spmd(nc, [arrays], core_ids=[0]).results[0]["out_acc"]
    return got[:T].reshape(IMAGES, SEQ, D)
```
